# Optimizing a Trainium2 kernel written in Bass

```python
import numpy as np
import jax
import jax.numpy as jnp

def _softmax(x, axis=-1):
    return jax.nn.softmax(x, axis=axis)

def _gelu(x):
    return jax.nn.gelu(x, approximate=True)

def _silu(x):
    return jax.nn.silu(x)

def _sigmoid(x):
    return jax.nn.sigmoid(x)

def _layernorm(x, axis=-1, eps=1e-05):
    m = jnp.mean(x, axis=axis, keepdims=True)
    v = jnp.var(x, axis=axis, keepdims=True)
    return (x - m) / jnp.sqrt(v + eps)

def _scatter_add(tgt, idx, src, axis=0):
    return tgt.at[idx].add(src)

def _segment_sum(src, seg, n):
    return jax.ops.segment_sum(src, seg, n)
kernel_name = 'mk_seq_preln_d1_jaxref_r8_750070'

def setup_inputs(seed: int=0):
    np.random.seed(seed)
    _w = jnp.asarray

    def _L0_attn_setup():
        import jax, jax.numpy as jnp
        import numpy as np
        B, T, D = (4, 256, 128)
        DIN = 2 * D
        SIGN = jnp.array([1.0, -1.0, -1.0, -1.0, -1.0, -1.0, -1.0, -1.0], dtype=jnp.float32)

        def _ln(v, w, b, eps=1e-05):
            m = v.mean(-1, keepdims=True)
            va = ((v - m) ** 2).mean(-1, keepdims=True)
            return (v - m) / jnp.sqrt(va + eps) * w + b

        def _reference_tuple_inner(x, W_in, b_in, basis_real, basis_imag, ln_w, ln_b, theta, omega, sigma, W_sp, b_sp, W_g, b_g, W_out, b_out, norm_w, norm_b):
            x_inner = x @ W_in + b_in
            wr = x_inner @ basis_real
            wi = x_inner @ basis_imag
            vec = _ln(jnp.concatenate([wr, wi], -1), ln_w, ln_b)
            wr, wi = (vec[..., :8], vec[..., 8:])
            cos_t, sin_t = (jnp.cos(theta), jnp.sin(theta))
            scale = jnp.clip(sigma, 0.5, 2.0) * (1.0 + 0.1 * omega)

            def step(carry, w):
                hr, hi = carry
                cr, ci = w
                rr = (hr * cos_t - hi * sin_t) * scale
                ri = (hr * sin_t + hi * cos_t) * scale
                a, b_ = (rr[:, :4], rr[:, 4:])
                ai, bi = (ri[:, :4], ri[:, 4:])
                c, d = (cr[:, :4], cr[:, 4:])
                c2, d2 = (ci[:, :4], ci[:, 4:])
                nr = jnp.concatenate([a * c - d * b_, ai * c2 - d2 * bi], -1)
                ni = jnp.concatenate([d * a + b_ * c, d2 * ai + bi * c2], -1)
                return ((nr, ni), (nr, ni))
            bsz = x.shape[0]
            init = (jnp.zeros((bsz, 8), x.dtype), jnp.zeros((bsz, 8), x.dtype))
            (hr_f, hi_f), (Rs, Is) = jax.lax.scan(step, init, (wr.transpose(1, 0, 2), wi.transpose(1, 0, 2)))
            Rs = Rs.transpose(1, 0, 2)
            Is = Is.transpose(1, 0, 2)
            inv = SIGN * (Rs ** 2 + Is ** 2)
            y = inv @ W_sp + b_sp
            g = jax.nn.silu(x_inner @ W_g + b_g)
            out = y * g @ W_out + b_out
            out = _ln(x + out, norm_w, norm_b)
            final_state = jnp.concatenate([hr_f, hi_f], -1)
            return (out, final_state)
        key = jax.random.key(seed)
        ks = jax.random.split(key, 18)
        s = 1.0 / np.sqrt(D)
        si = 1.0 / np.sqrt(DIN)
        return {'x': jax.random.normal(ks[0], (B, T, D), jnp.float32), 'W_in': jax.random.normal(ks[1], (D, DIN), jnp.float32) * s, 'b_in': jnp.zeros((DIN,), jnp.float32), 'basis_real': jax.random.normal(ks[2], (DIN, 8), jnp.float32) * si, 'basis_imag': jax.random.normal(ks[3], (DIN, 8), jnp.float32) * si, 'ln_w': jnp.ones((16,), jnp.float32), 'ln_b': jnp.zeros((16,), jnp.float32), 'theta': jax.random.normal(ks[4], (8,), jnp.float32) * 0.1, 'omega': jax.random.normal(ks[5], (8,), jnp.float32) * 0.1, 'sigma': jnp.ones((8,), jnp.float32), 'W_sp': jax.random.normal(ks[6], (8, DIN), jnp.float32) * (1.0 / np.sqrt(8)), 'b_sp': jnp.zeros((DIN,), jnp.float32), 'W_g': jax.random.normal(ks[7], (DIN, DIN), jnp.float32) * si, 'b_g': jnp.zeros((DIN,), jnp.float32), 'W_out': jax.random.normal(ks[8], (DIN, D), jnp.float32) * si, 'b_out': jnp.zeros((D,), jnp.float32), 'norm_w': jnp.ones((D,), jnp.float32), 'norm_b': jnp.zeros((D,), jnp.float32)}
    _L0_attn_in = _L0_attn_setup()

    def _L0_ffn_setup():
        import jax, jax.numpy as jnp
        import numpy as np
        D_MODEL = 128
        N_HEADS = 16
        N_EXPERTS = 8
        TOP_K = 2
        EXPERT_HIDDEN = D_MODEL * 4 // N_EXPERTS

        def layer_norm(x, g, b, eps=1e-05):
            mu = jnp.mean(x, axis=-1, keepdims=True)
            var = jnp.var(x, axis=-1, keepdims=True)
            return (x - mu) * jax.lax.rsqrt(var + eps) * g + b
        key = jax.random.key(seed)
        ks = jax.random.split(key, 12)
        s = 1.0 / np.sqrt(D_MODEL)
        return {'x': jax.random.normal(ks[0], (2, 256, D_MODEL), dtype=jnp.float32), 'Wq': jax.random.normal(ks[1], (D_MODEL, D_MODEL), dtype=jnp.float32) * s, 'Wk': jax.random.normal(ks[2], (D_MODEL, D_MODEL), dtype=jnp.float32) * s, 'Wv': jax.random.normal(ks[3], (D_MODEL, D_MODEL), dtype=jnp.float32) * s, 'Wo': jax.random.normal(ks[4], (D_MODEL, D_MODEL), dtype=jnp.float32) * s, 'g1': jnp.ones((D_MODEL,), jnp.float32), 'b1': jnp.zeros((D_MODEL,), jnp.float32), 'g2': jnp.ones((D_MODEL,), jnp.float32), 'b2': jnp.zeros((D_MODEL,), jnp.float32), 'Wg': jax.random.normal(ks[5], (D_MODEL, N_EXPERTS), dtype=jnp.float32) * s, 'W1': jax.random.normal(ks[6], (N_EXPERTS, D_MODEL, EXPERT_HIDDEN), dtype=jnp.float32) * s, 'W2': jax.random.normal(ks[7], (N_EXPERTS, EXPERT_HIDDEN, D_MODEL), dtype=jnp.float32) * (1.0 / np.sqrt(EXPERT_HIDDEN))}
    _L0_ffn_in = _L0_ffn_setup()
    _d = {'L0_attn_x': _L0_attn_in['x'], 'L0_attn_W_in': _L0_attn_in['W_in'], 'L0_attn_b_in': _L0_attn_in['b_in'], 'L0_attn_basis_real': _L0_attn_in['basis_real'], 'L0_attn_basis_imag': _L0_attn_in['basis_imag'], 'L0_attn_ln_w': _L0_attn_in['ln_w'], 'L0_attn_ln_b': _L0_attn_in['ln_b'], 'L0_attn_theta': _L0_attn_in['theta'], 'L0_attn_omega': _L0_attn_in['omega'], 'L0_attn_sigma': _L0_attn_in['sigma'], 'L0_attn_W_sp': _L0_attn_in['W_sp'], 'L0_attn_b_sp': _L0_attn_in['b_sp'], 'L0_attn_W_g': _L0_attn_in['W_g'], 'L0_attn_b_g': _L0_attn_in['b_g'], 'L0_attn_W_out': _L0_attn_in['W_out'], 'L0_attn_b_out': _L0_attn_in['b_out'], 'L0_attn_norm_w': _L0_attn_in['norm_w'], 'L0_attn_norm_b': _L0_attn_in['norm_b'], 'L0_ffn_Wq': _L0_ffn_in['Wq'], 'L0_ffn_Wk': _L0_ffn_in['Wk'], 'L0_ffn_Wv': _L0_ffn_in['Wv'], 'L0_ffn_Wo': _L0_ffn_in['Wo'], 'L0_ffn_g1': _L0_ffn_in['g1'], 'L0_ffn_b1': _L0_ffn_in['b1'], 'L0_ffn_g2': _L0_ffn_in['g2'], 'L0_ffn_b2': _L0_ffn_in['b2'], 'L0_ffn_Wg': _L0_ffn_in['Wg'], 'L0_ffn_W1': _L0_ffn_in['W1'], 'L0_ffn_W2': _L0_ffn_in['W2']}
    _x0 = _d['L0_attn_x']
    _d['L0_attn_x'] = jax.random.normal(jax.random.fold_in(jax.random.key(seed), 1), (32, 256, 128), dtype=_x0.dtype)
    del _x0
    return _d

def reference(L0_attn_x, L0_attn_W_in, L0_attn_b_in, L0_attn_basis_real, L0_attn_basis_imag, L0_attn_ln_w, L0_attn_ln_b, L0_attn_theta, L0_attn_omega, L0_attn_sigma, L0_attn_W_sp, L0_attn_b_sp, L0_attn_W_g, L0_attn_b_g, L0_attn_W_out, L0_attn_b_out, L0_attn_norm_w, L0_attn_norm_b, L0_ffn_Wq, L0_ffn_Wk, L0_ffn_Wv, L0_ffn_Wo, L0_ffn_g1, L0_ffn_b1, L0_ffn_g2, L0_ffn_b2, L0_ffn_Wg, L0_ffn_W1, L0_ffn_W2):

    def _L0_attn_ref(x, W_in, b_in, basis_real, basis_imag, ln_w, ln_b, theta, omega, sigma, W_sp, b_sp, W_g, b_g, W_out, b_out, norm_w, norm_b):
        import jax, jax.numpy as jnp
        import numpy as np
        B, T, D = (4, 256, 128)
        DIN = 2 * D
        SIGN = jnp.array([1.0, -1.0, -1.0, -1.0, -1.0, -1.0, -1.0, -1.0], dtype=jnp.float32)

        def _ln(v, w, b, eps=1e-05):
            m = v.mean(-1, keepdims=True)
            va = ((v - m) ** 2).mean(-1, keepdims=True)
            return (v - m) / jnp.sqrt(va + eps) * w + b

        def _reference_tuple_inner(x, W_in, b_in, basis_real, basis_imag, ln_w, ln_b, theta, omega, sigma, W_sp, b_sp, W_g, b_g, W_out, b_out, norm_w, norm_b):
            x_inner = x @ W_in + b_in
            wr = x_inner @ basis_real
            wi = x_inner @ basis_imag
            vec = _ln(jnp.concatenate([wr, wi], -1), ln_w, ln_b)
            wr, wi = (vec[..., :8], vec[..., 8:])
            cos_t, sin_t = (jnp.cos(theta), jnp.sin(theta))
            scale = jnp.clip(sigma, 0.5, 2.0) * (1.0 + 0.1 * omega)

            def step(carry, w):
                hr, hi = carry
                cr, ci = w
                rr = (hr * cos_t - hi * sin_t) * scale
                ri = (hr * sin_t + hi * cos_t) * scale
                a, b_ = (rr[:, :4], rr[:, 4:])
                ai, bi = (ri[:, :4], ri[:, 4:])
                c, d = (cr[:, :4], cr[:, 4:])
                c2, d2 = (ci[:, :4], ci[:, 4:])
                nr = jnp.concatenate([a * c - d * b_, ai * c2 - d2 * bi], -1)
                ni = jnp.concatenate([d * a + b_ * c, d2 * ai + bi * c2], -1)
                return ((nr, ni), (nr, ni))
            bsz = x.shape[0]
            init = (jnp.zeros((bsz, 8), x.dtype), jnp.zeros((bsz, 8), x.dtype))
            (hr_f, hi_f), (Rs, Is) = jax.lax.scan(step, init, (wr.transpose(1, 0, 2), wi.transpose(1, 0, 2)))
            Rs = Rs.transpose(1, 0, 2)
            Is = Is.transpose(1, 0, 2)
            inv = SIGN * (Rs ** 2 + Is ** 2)
            y = inv @ W_sp + b_sp
            g = jax.nn.silu(x_inner @ W_g + b_g)
            out = y * g @ W_out + b_out
            out = _ln(x + out, norm_w, norm_b)
            final_state = jnp.concatenate([hr_f, hi_f], -1)
            return (out, final_state)
        return _reference_tuple_inner(x, W_in, b_in, basis_real, basis_imag, ln_w, ln_b, theta, omega, sigma, W_sp, b_sp, W_g, b_g, W_out, b_out, norm_w, norm_b)[0]

    def _L0_ffn_ref(x, Wq, Wk, Wv, Wo, g1, b1, g2, b2, Wg, W1, W2):
        import jax, jax.numpy as jnp
        import numpy as np
        D_MODEL = 128
        N_HEADS = 16
        N_EXPERTS = 8
        TOP_K = 2
        EXPERT_HIDDEN = D_MODEL * 4 // N_EXPERTS

        def layer_norm(x, g, b, eps=1e-05):
            mu = jnp.mean(x, axis=-1, keepdims=True)
            var = jnp.var(x, axis=-1, keepdims=True)
            return (x - mu) * jax.lax.rsqrt(var + eps) * g + b
        B, S, D = x.shape
        H, dk = (N_HEADS, D // N_HEADS)
        xn = layer_norm(x, g1, b1)
        q = (xn @ Wq).reshape(B, S, H, dk).transpose(0, 2, 1, 3)
        k = (xn @ Wk).reshape(B, S, H, dk).transpose(0, 2, 1, 3)
        v = (xn @ Wv).reshape(B, S, H, dk).transpose(0, 2, 1, 3)
        scores = jnp.einsum('bhqd,bhkd->bhqk', q, k) / np.sqrt(dk)
        attn = jax.nn.softmax(scores, axis=-1)
        o = jnp.einsum('bhqk,bhkd->bhqd', attn, v)
        o = o.transpose(0, 2, 1, 3).reshape(B, S, D) @ Wo
        x = x + o
        xn2 = layer_norm(x, g2, b2)
        xf = xn2.reshape(B * S, D)
        gate = xf @ Wg
        topv, topi = jax.lax.top_k(gate, TOP_K)
        probs = jax.nn.softmax(topv, axis=-1)
        cw = jnp.sum(jax.nn.one_hot(topi, N_EXPERTS, dtype=xf.dtype) * probs[..., None], axis=1)
        h = jax.nn.relu(jnp.einsum('td,edh->teh', xf, W1))
        y = jnp.einsum('teh,ehd->ted', h, W2)
        moe = jnp.einsum('ted,te->td', y, cw).reshape(B, S, D)
        return x + moe
    x = L0_attn_x
    x = x + _L0_attn_ref(_layernorm(x, axis=-1), L0_attn_W_in, L0_attn_b_in, L0_attn_basis_real, L0_attn_basis_imag, L0_attn_ln_w, L0_attn_ln_b, L0_attn_theta, L0_attn_omega, L0_attn_sigma, L0_attn_W_sp, L0_attn_b_sp, L0_attn_W_g, L0_attn_b_g, L0_attn_W_out, L0_attn_b_out, L0_attn_norm_w, L0_attn_norm_b)
    x = x + _L0_ffn_ref(_layernorm(x, axis=-1), L0_ffn_Wq, L0_ffn_Wk, L0_ffn_Wv, L0_ffn_Wo, L0_ffn_g1, L0_ffn_b1, L0_ffn_g2, L0_ffn_b2, L0_ffn_Wg, L0_ffn_W1, L0_ffn_W2)
    return x

_drawn_inputs = setup_inputs


def setup_inputs(seed=0):
    import zlib

    import numpy as np

    out = dict(_drawn_inputs(seed))
    spreads = {'L0_attn_b_in': (0.0, 0.8),
     'L0_attn_ln_w': (1.0, 0.2),
     'L0_attn_ln_b': (0.0, 0.1),
     'L0_attn_sigma': (1.0, 0.2),
     'L0_attn_b_sp': (0.0, 0.1),
     'L0_attn_b_g': (0.0, 0.8),
     'L0_attn_b_out': (0.0, 0.1),
     'L0_attn_norm_w': (1.0, 0.2),
     'L0_attn_norm_b': (0.0, 0.1),
     'L0_ffn_g1': (1.0, 0.2),
     'L0_ffn_b1': (0.0, 0.1),
     'L0_ffn_g2': (1.0, 0.2),
     'L0_ffn_b2': (0.0, 0.1)}
    factors = {}
    for name, (base, spread) in spreads.items():
        noise = np.random.default_rng([zlib.crc32(name.encode()), seed]).standard_normal(out[name].shape)
        drawn = base * np.exp(spread * noise) if base else spread * noise
        out[name] = jnp.asarray(drawn.astype(out[name].dtype))
    for name, factor in factors.items():
        out[name] = (out[name] * factor).astype(out[name].dtype)
    return out
```

```python
from contextlib import ExitStack

import concourse.bass as bass
from concourse import mybir

F32 = mybir.dt.float32
BF16 = mybir.dt.bfloat16
U32 = mybir.dt.uint32
ALU = mybir.AluOpType
ACT = mybir.ActivationFunctionType
AX_X = mybir.AxisListType.X
EPS = 1e-5

P = 128
HEADS = 16
GROUP = 4
GROUPS = HEADS // GROUP
TERMS = ((0, 0), (0, 1), (1, 0), (0, 2), (2, 0), (1, 1))
PART_ROW = 32
SHIFT_ROW = PART_ROW + 8 * len(TERMS)
STACK_ROWS = SHIFT_ROW + 2
UNROLL = 4
P_RING = 8
GATE_COLS = 96


class Batch:

    def __init__(self, turn, offset):
        self.turn, self.offset = turn, offset

    def ago(self, n):
        return Batch(self.turn, self.offset - n)

    def past(self, n):
        return self.turn is not None or self.offset >= n

    def turnof(self, n):
        return self.offset % n

    def index(self):
        return self.offset if self.turn is None else self.turn * UNROLL + self.offset


class Count:

    def __init__(self, sem, per, every=1):
        self.sem, self.per, self.every = sem, per, every

    def at(self, b, n=None):
        value = self.per * (b.offset // self.every) + (self.per if n is None else n)
        assert value > 0
        if b.turn is None:
            return value
        return b.turn * (self.per * (UNROLL // self.every)) + value


def build(nc, x, W_in, b_in, W_sp_bias, W_g, b_g, W_out, b_out, norm_w, norm_b,
          Wq, Wk, Wv, Wo, g1, b1, g2, b2, Wgate, W1, W2, out):
    B, T, D = x.shape
    TT = T // P
    DIN = W_in.shape[1]
    FB = DIN // P
    DK = D // HEADS
    E, _, EH = W1.shape
    HB = E * EH // P
    EPB = P // EH
    N = T
    assert D == P and TT == 2 and DIN == 2 * P and DK == 8 and EPB == 2 and E == 8
    SCALE = float(DK) ** -0.5

    with ExitStack() as ctx:
        def sb(name, shape, dt=F32):
            return ctx.enter_context(nc.sbuf_tensor(name, shape, dt))

        def bank(name):
            return ctx.enter_context(nc.psum_tensor(name, [P, 512], F32))

        def sem(name):
            return ctx.enter_context(nc.semaphore(name))

        def count(name, per, every=1):
            if every == 1:
                return Count(sem(name), per)
            return [Count(sem(f"{name}{k}"), per, every) for k in range(every)]

        ident = sb("ident", [P, P])
        minus_half = sb("minus_half", [P, 2 * TT])
        iota_e = sb("iota_e", [P, E])
        w_in = sb("w_in", [P, DIN])
        w_inT = sb("w_inT", [P, FB, P])
        w_g = sb("w_g", [P, FB, DIN])
        b_in_c = sb("b_in_c", [P, FB])
        b_g_c = sb("b_g_c", [P, FB])
        b_sp_c = sb("b_sp_c", [P, FB])
        w_z = sb("w_z", [P, DIN])
        b_z = sb("b_z", [P, FB])
        b_z_half = sb("b_z_half", [P, FB])
        w_out = sb("w_out", [P, FB, D])
        w_outs = sb("w_outs", [P, FB, D])
        b_out_r = sb("b_out_r", [P, D])
        norm_w_r = sb("norm_w_r", [P, D])
        norm_b_r = sb("norm_b_r", [P, D])
        w_qkv = sb("w_qkv", [P, 3, D])
        w_qkvs = sb("w_qkvs", [P, 3, D])
        w_o = sb("w_o", [P, D])
        g1_c = sb("g1_c", [P, 1])
        b1_c = sb("b1_c", [P, 1])
        g2_c = sb("g2_c", [P, 1])
        b2_c = sb("b2_c", [P, 1])
        b_qk = sb("b_qk", [P, 2])
        b_v = sb("b_v", [P, 1])
        ones = sb("ones", [P, P])
        b_v_wide = sb("b_v_wide", [P, P])
        b2_wide = sb("b2_wide", [P, P])
        c_row = sb("c_row", [P, D])
        w_gate = sb("w_gate", [P, E])
        w_gates = sb("w_gates", [P, GATE_COLS])
        b_gate_r = sb("b_gate_r", [P, E])
        w_1 = sb("w_1", [P, E, EH])
        w_1s = sb("w_1s", [P, E * EH])
        b_1 = sb("b_1", [P, HB])
        w_2 = sb("w_2", [P, HB, D])

        xin = sb("xin", [P, 2, TT, D])
        stats1 = sb("stats1", [P, TT, 6])
        mv1 = sb("mv1", [P, TT, 2])
        ve1 = sb("ve1", [P, TT])
        rstd1 = sb("rstd1", [P, TT])
        L = sb("L", [P, 2, TT, D])
        Lb = sb("Lb", [P, TT, D])
        xb = sb("xb", [P, 2, TT, D])
        LT = sb("LT", [P, N])
        th = sb("th", [P, FB, N])
        sg = sb("sg", [P, FB, N])
        gT = sb("gT", [P, FB, N])
        r = sb("r", [P, 2, TT, D])
        stats2 = sb("stats2", [P, TT, 6])
        mv2 = sb("mv2", [P, TT, 2])
        ve2 = sb("ve2", [P, TT])
        rstd2 = sb("rstd2", [P, TT])
        a = sb("a", [P, TT, D])
        aw = sb("aw", [P, TT, D])
        x1 = sb("x1", [P, 2, TT, D])
        x1_kept = sb("x1_kept", [P, 4, TT, D])
        stats3 = sb("stats3", [P, TT, 6])
        mv3 = sb("mv3", [P, 2, TT, 2])
        ve3 = sb("ve3", [P, 2, TT])
        rstd3 = sb("rstd3", [P, 2, 2, TT])
        n3 = sb("n3", [P, TT, D])
        L3 = sb("L3", [P, TT, D])
        L3c = sb("L3c", [P, 4, TT, D])
        nT = sb("nT", [P, N])
        qk = sb("qk", [P, 2, N])
        rest = sb("rest", [P, 2, N])
        parts = sb("parts", [P, 3, 2, N], BF16)
        q_stack = [sb(f"q_stack{k}", [STACK_ROWS, HEADS, N], BF16) for k in range(4)]
        k_stack = [sb(f"k_stack{k}", [STACK_ROWS, HEADS, N], BF16) for k in range(4)]
        v_one = sb("v_one", [P, 4, TT, HEADS, 32])
        neg_max = sb("neg_max", [P, 2, TT, HEADS])
        max_hi = sb("max_hi", [HEADS // 2, 2, N], BF16)
        max_lo = sb("max_lo", [HEADS // 2, 2, N], BF16)
        probs = sb("probs", [P, P_RING, TT, N])
        oT = sb("oT", [P, GROUPS, N])
        r_sum = sb("r_sum", [P, TT, HEADS])
        on = sb("on", [P, TT, HEADS, DK])
        onT = sb("onT", [P, N])
        x2 = sb("x2", [P, 2, TT, D])
        x12 = sb("x12", [P, 4, TT, D])
        stats4 = sb("stats4", [P, TT, 6])
        mv4 = sb("mv4", [P, TT, 2])
        ve4 = sb("ve4", [P, TT])
        rstd4 = sb("rstd4", [P, TT])
        n4 = sb("n4", [P, TT, D])
        n4T = sb("n4T", [P, 2, N])
        gate = sb("gate", [P, TT, E])
        top = sb("top", [P, TT, 8])
        top_at = sb("top_at", [P, TT, 8], U32)
        top_atf = sb("top_atf", [P, TT, 8])
        gap = sb("gap", [P, TT])
        e_gap = sb("e_gap", [P, TT])
        denom = sb("denom", [P, TT])
        prob2 = sb("prob2", [P, 2, TT])
        pick = sb("pick", [P, 2, TT, E])
        mix_w = sb("mix_w", [P, TT, E])
        mix_wT = sb("mix_wT", [E, N])
        mix_wide = sb("mix_wide", [P, HB, N])
        hid = sb("hid", [P, HB, N])
        hidw = sb("hidw", [P, HB, N])
        ob = sb("ob", [P, TT, D])
        mix_dram = nc.dram_tensor("mix_dram", [E, N], F32, kind="Internal").ap()

        bank_s = [bank(f"bank_s{k}") for k in range(2)]
        bank_m = [bank(f"bank_m{k}") for k in range(2)]
        bank_o = bank("bank_o")
        bank_a = bank("bank_a")
        bank_c = bank("bank_c")
        bank_d = bank("bank_d")

        carrier = sem("carrier")
        s_load = sem("s_load")
        s_const = sem("s_const")
        s_zero = sem("s_zero")
        s_set = sem("s_set")
        s_fold_v = sem("s_fold_v")
        s_fold_p = sem("s_fold_p")
        x_in = count("x_in", 16, 2)
        st1 = count("st1", TT)
        mv1_ok = count("mv1_ok", TT)
        ve1_ok = count("ve1_ok", 1)
        rstd1_ok = count("rstd1_ok", 1)
        L_ok = count("L_ok", TT)
        Lb_ok = count("Lb_ok", 1)
        xb_ok = count("xb_ok", 1)
        LT_up = count("LT_up", 1)
        LT_ok = count("LT_ok", 1)
        z_up = count("z_up", 1)
        th_ok = count("th_ok", FB)
        sg_ok = count("sg_ok", 1)
        gT_ok = count("gT_ok", FB)
        o_up = count("o_up", 1)
        r_ok = count("r_ok", 1)
        st2 = count("st2", TT)
        mv2_ok = count("mv2_ok", TT)
        ve2_ok = count("ve2_ok", 1)
        rstd2_ok = count("rstd2_ok", 1)
        a_ok = count("a_ok", TT)
        x1_ok = count("x1_ok", 2)
        st3 = count("st3", TT)
        mv3_ok = count("mv3_ok", TT)
        ve3_ok = count("ve3_ok", 2)
        rstd3_ok = count("rstd3_ok", 1)
        n3_ok = count("n3_ok", TT)
        L3_ok = count("L3_ok", TT)
        kept = count("kept", 1)
        L3c_ok = count("L3c_ok", 1)
        nT_up = count("nT_up", 1)
        nT_ok = count("nT_ok", 1)
        qk_up = count("qk_up", 1)
        qk_ok = count("qk_ok", 2)
        v_up = count("v_up", 1)
        v_ok = count("v_ok", 1)
        hi_ok = count("hi_ok", 1)
        rest_ok = count("rest_ok", 1)
        mid_ok = count("mid_ok", 1)
        low_ok = count("low_ok", 1)
        stacked = count("stacked", 16 * 2 * len(TERMS), 2)
        m_up = count("m_up", HEADS)
        m_ok = count("m_ok", HEADS)
        mT_up = count("mT_up", 2)
        mhi_ok = count("mhi_ok", 2)
        mlo_ok = count("mlo_ok", 2)
        shift_in = [count(f"shift_in{half}_", 32, 2) for half in range(2)]
        s_up = count("s_up", HEADS)
        p_ok = count("p_ok", HEADS)
        pv_up = count("pv_up", GROUPS)
        oT_ok = count("oT_ok", 2)
        tok_up = count("tok_up", TT)
        rs_ok = count("rs_ok", TT)
        on_ok = count("on_ok", TT)
        onT_up = count("onT_up", 1)
        onT_ok = count("onT_ok", 1)
        att_up = count("att_up", 1)
        x2_ok = count("x2_ok", 1)
        x12_ok = count("x12_ok", 1)
        st4 = count("st4", TT)
        mv4_ok = count("mv4_ok", TT)
        ve4_ok = count("ve4_ok", 1)
        rstd4_ok = count("rstd4_ok", 1)
        n4_ok = count("n4_ok", TT)
        n4T_up = count("n4T_up", 1)
        n4T_ok = count("n4T_ok", 1)
        gate_up = count("gate_up", 1)
        gate_ok = count("gate_ok", 1)
        top_ok = count("top_ok", TT)
        at_ok = count("at_ok", TT)
        atf_ok = count("atf_ok", 1)
        gap_ok = count("gap_ok", 1)
        eg_ok = count("eg_ok", 1)
        den_ok = count("den_ok", 1)
        p1_ok = count("p1_ok", 1)
        p2_ok = count("p2_ok", 1)
        pick_ok = count("pick_ok", 2 * TT)
        mw_ok = count("mw_ok", 1)
        mwT_up = count("mwT_up", 1)
        mwT_ok = count("mwT_ok", 1)
        mw_out = count("mw_out", 16)
        mw_wide = count("mw_wide", 32)
        h_up = count("h_up", HB // 2)
        h_ok = count("h_ok", HB)
        hw_ok = count("hw_ok", 1)
        y_up = count("y_up", 1)
        ob_ok = count("ob_ok", 1)
        o_out = count("o_out", 16)

        FIRST, LOOP0 = -4, 4
        TURNS = (B - 4 - LOOP0) // UNROLL
        AFTER = LOOP0 + UNROLL * TURNS
        LAST = B + 3

        def slots(eng, slot):
            def batches(s, turn=None):
                def at(ahead):
                    b = s + ahead
                    return Batch(turn, b) if turn is not None or 0 <= b < B else None
                return at

            for s in range(FIRST, LOOP0):
                slot(batches(s))
            with eng.Fori(0, TURNS) as turn:
                for u in range(UNROLL):
                    slot(batches(LOOP0 + u, turn))
            for s in range(AFTER, LAST):
                slot(batches(s))

        def carry(eng, b):
            if b.turn is not None:
                eng.sem_inc(carrier, 1)

        block = ctx.enter_context(nc.Block())

        @block.sync
        def _(eng):
            def row(v):
                return v.rearrange("(o n) -> o n", o=1).broadcast_to([P, v.shape[0]])

            def cols(v):
                return v.rearrange("(c p) -> p c", p=P)

            loads = [
                (w_in[:, :], W_in), (w_g[:, :, :], W_g.rearrange("(j p) n -> p j n", p=P)),
                (b_in_c[:, :], cols(b_in)), (b_g_c[:, :], cols(b_g)), (b_sp_c[:, :], cols(W_sp_bias)),
                (w_out[:, :, :], W_out.rearrange("(j p) n -> p j n", p=P)),
                (b_out_r[:, :], row(b_out)), (norm_w_r[:, :], row(norm_w)), (norm_b_r[:, :], row(norm_b)),
                (w_qkv[:, 0, :], Wq), (w_qkv[:, 1, :], Wk), (w_qkv[:, 2, :], Wv), (w_o[:, :], Wo),
                (g1_c[:, :], cols(g1)), (b1_c[:, :], cols(b1)), (g2_c[:, :], cols(g2)), (b2_c[:, :], cols(b2)),
                (w_gate[:, :], Wgate), (w_1[:, :, :], W1.rearrange("e d h -> d e h")),
                (w_2[:, :, :], W2.rearrange("(j o) h d -> (o h) j d", o=EPB)),
            ]
            for to, of in loads:
                eng.dma_start(to, of, allow_slow_non_contiguous=True).then_inc(s_load, 16)
            assert len(loads) == LOADS

            def slot(at):
                b = at(0)
                if b:
                    shift(b, 0)
                b = at(4)
                if b:
                    k = b.turnof(2)
                    if b.past(2):
                        eng.wait_ge(xb_ok.sem, xb_ok.at(b.ago(2)))
                        carry(eng, b)
                        eng.wait_ge(L_ok.sem, L_ok.at(b.ago(2)))
                        carry(eng, b)
                    eng.dma_start(xin[:, k, :, :], x[b.index(), :, :].rearrange("(t p) d -> p t d", p=P))\
                       .then_inc(x_in[k].sem, 16)
                b = at(1)
                if b:
                    eng.wait_ge(low_ok.sem, low_ok.at(b))
                    carry(eng, b)
                    stack_up(b, 2)
                b = at(-3)
                if b:
                    eng.wait_ge(mwT_ok.sem, mwT_ok.at(b))
                    carry(eng, b)
                    if b.past(1):
                        eng.wait_ge(mw_wide.sem, mw_wide.at(b.ago(1)))
                        carry(eng, b)
                    eng.dma_start(mix_dram, mix_wT[:, :]).then_inc(mw_out.sem, 16)
                    eng.wait_ge(mw_out.sem, mw_out.at(b))
                    carry(eng, b)
                    if b.past(1):
                        eng.wait_ge(hw_ok.sem, hw_ok.at(b.ago(1)))
                        carry(eng, b)
                    src = mix_dram.rearrange("(j o) n -> o j n", o=EPB)
                    for o in range(EPB):
                        eng.dma_start(mix_wide[o * EH:(o + 1) * EH, :, :],
                                      src[o:o + 1, :, :].broadcast_to([EH, HB, N])).then_inc(mw_wide.sem, 16)
                b = at(0)
                if b:
                    shift(b, 1)
                b = at(2)
                if b:
                    if b.turn is None and b.offset == 0:
                        eng.wait_ge(s_zero, SET_POOL)
                        eng.wait_ge(s_set, SET_VECTOR)
                    if b.past(4):
                        eng.wait_ge(s_up.sem, s_up.at(b.ago(4)))
                        carry(eng, b)
                        eng.wait_ge(m_up.sem, m_up.at(b.ago(4)))
                        carry(eng, b)
                    eng.wait_ge(hi_ok.sem, hi_ok.at(b))
                    carry(eng, b)
                    stack_up(b, 0)
                    eng.wait_ge(mid_ok.sem, mid_ok.at(b))
                    carry(eng, b)
                    stack_up(b, 1)
                b = at(-3)
                if b:
                    eng.wait_ge(ob_ok.sem, ob_ok.at(b))
                    carry(eng, b)
                    eng.dma_start(out[b.index(), :, :].rearrange("(t p) d -> p t d", p=P), ob[:, :, :])\
                       .then_inc(o_out.sem, 16)

            def stack_up(b, part):
                for t, pair in enumerate(TERMS):
                    for which, stack in enumerate((q_stack[b.turnof(4)], k_stack[b.turnof(4)])):
                        if pair[which] == part:
                            row = PART_ROW + DK * t
                            eng.dma_start(stack[row:row + DK, :, :], parts[:, part, which, :])\
                               .then_inc(stacked[b.turnof(2)].sem, 16)

            def shift(b, half):
                k4, k2 = b.turnof(4), b.turnof(2)
                eng.wait_ge(mlo_ok.sem, mlo_ok.at(b, half + 1))
                carry(eng, b)
                eng.wait_ge(mhi_ok.sem, mhi_ok.at(b, half + 1))
                carry(eng, b)
                if b.past(4):
                    eng.wait_ge(s_up.sem, s_up.at(b.ago(4)))
                    carry(eng, b)
                hs = slice(half * (HEADS // 2), (half + 1) * (HEADS // 2))
                eng.dma_start(q_stack[k4][SHIFT_ROW:SHIFT_ROW + 1, hs, :], max_hi[:, half, :])\
                   .then_inc(shift_in[half][k2].sem, 16)
                eng.dma_start(q_stack[k4][SHIFT_ROW + 1:SHIFT_ROW + 2, hs, :], max_lo[:, half, :])\
                   .then_inc(shift_in[half][k2].sem, 16)

            slots(eng, slot)
            eng.wait_ge(o_out.sem, o_out.at(Batch(None, B - 1)))

        @block.gpsimd
        def _(eng):
            eng.memset(ident[:, :], 0.0).then_inc(s_zero, 1)
            eng.wait_ge(s_zero, 1)
            eng.affine_select(out=ident[:, :], in_=ident[:, :], compare_op=ALU.not_equal, fill=1.0, base=0,
                              pattern=[[-1, P]], channel_multiplier=1).then_inc(s_const, 1)
            eng.memset(minus_half[:, :], -0.5).then_inc(s_const, 1)
            eng.memset(ones[:, :], 1.0).then_inc(s_const, 1)
            eng.iota(iota_e[:, :], pattern=[[1, E]], base=0, channel_multiplier=0,
                     allow_small_or_imprecise_dtypes=True).then_inc(s_const, 1)
            eng.wait_ge(s_const, 4)
            eng.memset(v_one[:, :, :, :, DK:32], 0.0).then_inc(s_zero, 1)
            eng.wait_ge(s_zero, 2)
            eng.memset(v_one[:, :, :, :, DK:DK + 1], 1.0).then_inc(s_zero, 1)
            eng.wait_ge(s_zero, 3)
            for done, k in enumerate(POOL_SETS, start=1):
                eng.memset(q_stack[k][0:PART_ROW, :, :].bitcast(U32), 0)
                eng.memset(k_stack[k][0:PART_ROW, :, :].bitcast(U32), 0)
                eng.memset(k_stack[k][64:STACK_ROWS, :, :], 1.0).then_inc(s_zero, 1)
                eng.wait_ge(s_zero, 3 + done)
            assert 3 + len(POOL_SETS) == SET_POOL
            eng.wait_ge(s_load, 16 * LOADS)

            def wide(v):
                return v[:, :].rearrange("p (o d) -> p o d", o=1).broadcast_to([P, TT, D])

            def slot(at):
                b = at(4)
                if b:
                    eng.wait_ge(ve1_ok.sem, ve1_ok.at(b))
                    if b.past(1):
                        eng.wait_ge(L_ok.sem, L_ok.at(b.ago(1)))
                    eng.tensor_tensor(rstd1[:, :], ve1[:, :], minus_half[:, 0:TT], ALU.pow).then_inc(rstd1_ok.sem, 1)
                b = at(3)
                if b:
                    eng.wait_ge(ve2_ok.sem, ve2_ok.at(b))
                    if b.past(1):
                        eng.wait_ge(a_ok.sem, a_ok.at(b.ago(1)))
                    eng.tensor_tensor(rstd2[:, :], ve2[:, :], minus_half[:, 0:TT], ALU.pow).then_inc(rstd2_ok.sem, 1)
                b = at(2)
                if b:
                    eng.wait_ge(hi_ok.sem, hi_ok.at(b))
                    if b.past(1):
                        eng.wait_ge(low_ok.sem, low_ok.at(b.ago(1)))
                        eng.wait_ge(mid_ok.sem, mid_ok.at(b.ago(1)))
                    eng.tensor_tensor(rest[:, :, :], qk[:, :, :], parts[:, 0, :, :], ALU.subtract)\
                       .then_inc(rest_ok.sem, 1)
                b = at(-3)
                if b:
                    eng.wait_ge(h_ok.sem, h_ok.at(b))
                    eng.wait_ge(mw_wide.sem, mw_wide.at(b))
                    if b.past(1):
                        eng.wait_ge(y_up.sem, y_up.at(b.ago(1)))
                    eng.tensor_tensor(hidw[:, :, :], hid[:, :, :], mix_wide[:, :, :], ALU.mult)\
                       .then_inc(hw_ok.sem, 1)
                b = at(3)
                if b:
                    k = b.turnof(2)
                    eng.wait_ge(a_ok.sem, a_ok.at(b))
                    if b.past(1):
                        eng.wait_ge(x1_ok.sem, x1_ok.at(b.ago(1)))
                    eng.tensor_tensor(aw[:, :, :], a[:, :, :], wide(norm_w_r), ALU.mult).then_inc(x1_ok.sem, 1)
                    eng.wait_ge(x1_ok.sem, x1_ok.at(b, 1))
                    eng.wait_ge(xb_ok.sem, xb_ok.at(b))
                    if b.past(2):
                        eng.wait_ge(kept.sem, kept.at(b.ago(2)))
                        eng.wait_ge(L3_ok.sem, L3_ok.at(b.ago(2)))
                        eng.wait_ge(n3_ok.sem, n3_ok.at(b.ago(2)))
                    eng.tensor_tensor(x1[:, k, :, :], aw[:, :, :], xb[:, k, :, :], ALU.add)\
                       .then_inc(x1_ok.sem, 1)
                b = at(4)
                if b:
                    k = b.turnof(2)
                    if b.past(2):
                        eng.wait_ge(x1_ok.sem, x1_ok.at(b.ago(2)))
                    eng.wait_ge(x_in[k].sem, x_in[k].at(b))
                    eng.tensor_tensor(xb[:, k, :, :], xin[:, k, :, :], wide(norm_b_r), ALU.add)\
                       .then_inc(xb_ok.sem, 1)
                    eng.wait_ge(L_ok.sem, L_ok.at(b))
                    if b.past(1):
                        eng.wait_ge(r_ok.sem, r_ok.at(b.ago(1)))
                    eng.tensor_tensor(Lb[:, :, :], L[:, k, :, :], wide(b_out_r), ALU.add)\
                       .then_inc(Lb_ok.sem, 1)
                    eng.wait_ge(th_ok.sem, th_ok.at(b))
                    if b.past(1):
                        eng.wait_ge(gT_ok.sem, gT_ok.at(b.ago(1)))
                    carry(eng, b)
                    eng.tensor_scalar(sg[:, :, :], th[:, :, :], 0.5, 0.5, ALU.mult, ALU.add)\
                       .then_inc(sg_ok.sem, 1)
                b = at(3)
                if b:
                    k = b.turnof(2)
                    eng.wait_ge(ve3_ok.sem, ve3_ok.at(b))
                    if b.past(2):
                        eng.wait_ge(n3_ok.sem, n3_ok.at(b.ago(2)))
                        eng.wait_ge(L3_ok.sem, L3_ok.at(b.ago(2)))
                    eng.tensor_tensor(rstd3[:, k, :, :].rearrange("p k t -> p (k t)"),
                                      ve3[:, :, :].rearrange("p k t -> p (k t)"), minus_half[:, 0:2 * TT],
                                      ALU.pow).then_inc(rstd3_ok.sem, 1)
                b = at(2)
                if b:
                    k4 = b.turnof(4)
                    eng.wait_ge(mid_ok.sem, mid_ok.at(b))
                    if b.past(1):
                        eng.wait_ge(stacked[b.ago(1).turnof(2)].sem, stacked[b.ago(1).turnof(2)].at(b.ago(1)))
                    eng.tensor_tensor(parts[:, 2, :, :], rest[:, :, :], parts[:, 1, :, :], ALU.subtract)\
                       .then_inc(low_ok.sem, 1)
                    eng.wait_ge(L3_ok.sem, L3_ok.at(b))
                    if b.past(4):
                        eng.wait_ge(x2_ok.sem, x2_ok.at(b.ago(4)))
                    eng.tensor_tensor(L3c[:, k4, :, :], L3[:, :, :], wide(c_row), ALU.add).then_inc(L3c_ok.sem, 1)
                b = at(-1)
                if b:
                    k4 = b.turnof(4)
                    eng.wait_ge(ve4_ok.sem, ve4_ok.at(b))
                    if b.past(1):
                        eng.wait_ge(n4_ok.sem, n4_ok.at(b.ago(1)))
                    eng.tensor_tensor(rstd4[:, :], ve4[:, :], minus_half[:, 0:TT], ALU.pow).then_inc(rstd4_ok.sem, 1)
                    eng.wait_ge(x2_ok.sem, x2_ok.at(b))
                    eng.wait_ge(kept.sem, kept.at(b))
                    if b.past(3):
                        eng.wait_ge(ob_ok.sem, ob_ok.at(b.ago(3)))
                    eng.tensor_tensor(x12[:, k4, :, :], x1_kept[:, k4, :, :], x2[:, b.turnof(2), :, :],
                                      ALU.add).then_inc(x12_ok.sem, 1)

            slots(eng, slot)

        @block.scalar
        def _(eng):
            eng.wait_ge(s_fold_v, FOLD_V)

            def slot(at):
                for h in range(HEADS):
                    b = at(2)
                    if b and h == 0:
                        eng.wait_ge(v_up.sem, v_up.at(b))
                        if b.past(4):
                            eng.wait_ge(pv_up.sem, pv_up.at(b.ago(4)))
                        if b.turn is None and b.offset == 0:
                            eng.wait_ge(s_zero, 3)
                        eng.activation(v_one[:, b.turnof(4), :, :, 0:DK],
                                       bank_a[:, 0:N].rearrange("p (t h d) -> p t h d", t=TT, h=HEADS),
                                       ACT.Copy).then_inc(v_ok.sem, 1)
                    b = at(0)
                    if b and h == 2:
                        max_high(b, 1)
                    if b and h == 11:
                        turn_copy(b, 0)
                    b = at(1)
                    if b and h == 10:
                        max_high(b, 0)
                    b = at(-1)
                    if b and h == 2:
                        turn_copy(b, 1)
                    if b and h == 8:
                        eng.wait_ge(onT_up.sem, onT_up.at(b))
                        if b.past(1):
                            eng.wait_ge(att_up.sem, att_up.at(b.ago(1)))
                        eng.activation(onT[:, :], bank_c[:, 0:N], ACT.Copy).then_inc(onT_ok.sem, 1)
                    b = at(4)
                    if b and h == 4:
                        eng.wait_ge(LT_up.sem, LT_up.at(b))
                        if b.past(1):
                            eng.wait_ge(z_up.sem, z_up.at(b.ago(1)))
                        eng.activation(LT[:, :], bank_a[:, 0:N], ACT.Copy).then_inc(LT_ok.sem, 1)
                    if b and h == 6:
                        eng.wait_ge(z_up.sem, z_up.at(b))
                        if b.past(1):
                            eng.wait_ge(sg_ok.sem, sg_ok.at(b.ago(1)))
                        for f in range(FB):
                            eng.activation(th[:, f, :], bank_a[:, f * N:(f + 1) * N], ACT.Tanh,
                                           bias=b_z_half[:, f:f + 1], scale=0.5).then_inc(th_ok.sem, 1)
                    b = at(3)
                    if b and h == 12:
                        eng.wait_ge(nT_up.sem, nT_up.at(b))
                        if b.past(1):
                            eng.wait_ge(qk_up.sem, qk_up.at(b.ago(1)))
                            eng.wait_ge(v_up.sem, v_up.at(b.ago(1)))
                        eng.activation(nT[:, :], bank_a[:, 0:N], ACT.Copy).then_inc(nT_ok.sem, 1)
                    if b and h == 14:
                        eng.wait_ge(qk_up.sem, qk_up.at(b))
                        if b.past(1):
                            eng.wait_ge(rest_ok.sem, rest_ok.at(b.ago(1)))
                            eng.wait_ge(hi_ok.sem, hi_ok.at(b.ago(1)))
                        for w in range(2):
                            eng.activation(qk[:, w, :], bank_a[:, w * N:(w + 1) * N], ACT.Identity,
                                           bias=b_qk[:, w:w + 1]).then_inc(qk_ok.sem, 1)
                    b = at(-2)
                    if b and h == 1:
                        eng.wait_ge(n4T_up.sem, n4T_up.at(b))
                        if b.past(2):
                            eng.wait_ge(h_up.sem, h_up.at(b.ago(2)))
                        eng.activation(n4T[:, b.turnof(2), :], bank_d[:, 0:N], ACT.Copy).then_inc(n4T_ok.sem, 1)
                    if b and h in (5, 7):
                        j0 = h - 5
                        eng.wait_ge(h_up.sem, h_up.at(b, j0 // 2 + 1))
                        if b.past(1):
                            eng.wait_ge(hw_ok.sem, hw_ok.at(b.ago(1)))
                        for j in (j0, j0 + 1):
                            eng.activation(hid[:, j, :], bank_d[:, (j - j0) * N:(j - j0 + 1) * N], ACT.Relu,
                                           bias=b_1[:, j:j + 1]).then_inc(h_ok.sem, 1)
                    if b and h == 13:
                        eng.wait_ge(mwT_up.sem, mwT_up.at(b))
                        if b.past(1):
                            eng.wait_ge(mw_out.sem, mw_out.at(b.ago(1)))
                        eng.activation(mix_wT[:, :], bank_d[0:E, 0:N], ACT.Copy).then_inc(mwT_ok.sem, 1)
                    b = at(0)
                    if b:
                        eng.wait_ge(s_up.sem, s_up.at(b, h + 1))
                        if b.past(1) or (h - P_RING) // GROUP + 1 > 0:
                            eng.wait_ge(pv_up.sem, pv_up.at(b, (h - P_RING) // GROUP + 1))
                        eng.activation(probs[:, h % P_RING, :, :], bank_s[h % 2][:, :], ACT.Exp)\
                           .then_inc(p_ok.sem, 1)
                    b = at(2)
                    if b and h == 1:
                        eng.wait_ge(x1_ok.sem, x1_ok.at(b))
                        if b.past(4):
                            eng.wait_ge(x12_ok.sem, x12_ok.at(b.ago(4)))
                        eng.activation(x1_kept[:, b.turnof(4), :, :], x1[:, b.turnof(2), :, :], ACT.Copy)\
                           .then_inc(kept.sem, 1)
                    if b and h == 5:
                        eng.wait_ge(rest_ok.sem, rest_ok.at(b))
                        eng.activation(parts[:, 1, :, :], rest[:, :, :], ACT.Copy).then_inc(mid_ok.sem, 1)
                    b = at(3)
                    if b and h == 15:
                        eng.wait_ge(qk_ok.sem, qk_ok.at(b))
                        if b.past(1):
                            eng.wait_ge(stacked[b.ago(1).turnof(2)].sem, stacked[b.ago(1).turnof(2)].at(b.ago(1)))
                        eng.activation(parts[:, 0, :, :], qk[:, :, :], ACT.Copy).then_inc(hi_ok.sem, 1)
                    b = at(-2)
                    if b and h == 7:
                        eng.wait_ge(gap_ok.sem, gap_ok.at(b))
                        if b.past(1):
                            eng.wait_ge(p2_ok.sem, p2_ok.at(b.ago(1)))
                        eng.activation(e_gap[:, :], gap[:, :], ACT.Exp).then_inc(eg_ok.sem, 1)

            def max_high(b, half):
                eng.wait_ge(mT_up.sem, mT_up.at(b, half + 1))
                if b.past(1):
                    eng.wait_ge(shift_in[half][b.turnof(2) ^ 1].sem, shift_in[half][b.turnof(2) ^ 1].at(b.ago(1)))
                eng.activation(max_hi[:, half, :], bank_c[0:HEADS // 2, 0:N], ACT.Copy).then_inc(mhi_ok.sem, 1)

            def turn_copy(b, u):
                eng.wait_ge(pv_up.sem, pv_up.at(b, 2 * u + 2))
                if b.past(1):
                    eng.wait_ge(tok_up.sem, tok_up.at(b.ago(1)))
                eng.activation(oT[:, 2 * u:2 * u + 2, :], bank_o[:, :], ACT.Copy).then_inc(oT_ok.sem, 1)

            slots(eng, slot)

        @block.vector
        def _(eng):
            steps = [0]

            def folded(ins):
                steps[0] += 1
                ins.then_inc(s_fold_v, 1)

            for k in VECTOR_SETS:
                eng.memset(q_stack[k][0:PART_ROW, :, :].bitcast(U32), 0)
                eng.memset(k_stack[k][0:PART_ROW, :, :].bitcast(U32), 0)
                eng.memset(k_stack[k][64:STACK_ROWS, :, :], 1.0).then_inc(s_set, 1)
            assert len(VECTOR_SETS) == SET_VECTOR
            eng.wait_ge(s_load, 16 * LOADS)
            eng.wait_ge(s_const, 4)
            for j in range(FB):
                folded(eng.tensor_scalar(w_outs[:, j, :], w_out[:, j, :], b_sp_c[:, j:j + 1], None, ALU.mult))
            for w in range(3):
                to = w_qkvs[:, w, :]
                of = w_qkv[:, w, :]
                if w < 2:
                    of = of.rearrange("p (h d) -> p d h", d=DK)
                    to = to.rearrange("p (d h) -> p d h", d=DK)
                folded(eng.tensor_scalar(to, of, g1_c[:, 0:1], SCALE if w == 0 else 1.0, ALU.mult, ALU.mult))
            folded(eng.tensor_scalar(w_1s[:, :], w_1[:, :, :].rearrange("p e h -> p (e h)"), g2_c[:, 0:1], None,
                                     ALU.mult))
            folded(eng.memset(w_gates[:, E:GATE_COLS], 0.0))
            folded(eng.tensor_scalar(w_gates[:, 0:E], w_gate[:, :], g2_c[:, 0:1], None, ALU.mult))
            folded(eng.tensor_scalar(b2_wide[:, :], ones[:, :], b2_c[:, 0:1], None, ALU.mult))
            for w in range(2):
                folded(eng.tensor_scalar(x1[:, 0, w, :].rearrange("p (d h) -> p d h", d=DK),
                                         w_qkv[:, w, :].rearrange("p (h d) -> p d h", d=DK), 1.0, None, ALU.mult))
            assert steps[0] == FOLD_READY
            eng.wait_ge(s_fold_p, 1)
            folded(eng.tensor_copy(w_inT[:, :, :].rearrange("p j n -> p (j n)"), bank_a[:, 0:DIN]))
            eng.wait_ge(s_fold_p, 2)
            folded(eng.tensor_copy(b_v[:, :], bank_d[:, 0:1]))
            eng.wait_ge(s_fold_v, steps[0])
            folded(eng.tensor_scalar(b_v_wide[:, :], ones[:, :], b_v[:, 0:1], None, ALU.mult))
            assert steps[0] == FOLD_V_WIDE
            folded(eng.tensor_tensor(b_z[:, :], bank_c[:, 0:FB], b_g_c[:, :], ALU.add))
            folded(eng.tensor_scalar(b_qk[:, 0:1], bank_c[:, FB:FB + 1], SCALE, None, ALU.mult))
            folded(eng.tensor_copy(b_qk[:, 1:2], bank_c[:, FB + 1:FB + 2]))
            folded(eng.tensor_copy(b_1[:, :], bank_c[:, FB + 2:FB + 2 + HB]))
            eng.wait_ge(s_fold_v, steps[0])
            folded(eng.tensor_scalar(b_z_half[:, :], b_z[:, :], 0.5, None, ALU.mult))
            eng.wait_ge(s_fold_p, 3)
            folded(eng.tensor_copy(w_z[:, :], bank_a[:, 0:DIN]))
            folded(eng.tensor_copy(c_row[:, :], bank_s[0][:, 0:D]))
            folded(eng.tensor_copy(b_gate_r[:, :], bank_s[0][:, D:D + E]))
            assert steps[0] == FOLD_V
            eng.wait_ge(s_fold_v, FOLD_V)

            def stats(src, st, st_ok, mv, ok, b):
                for t in range(TT):
                    eng.bn_stats(st[:, t, :], src[:, t, :]).then_inc(st_ok.sem, 1)
                for t in range(TT):
                    eng.wait_ge(st_ok.sem, st_ok.at(b, t + 1))
                    carry(eng, b)
                    eng.bn_aggr(mv[:, t, :], st[:, t, :]).then_inc(ok.sem, 1)

            def centred(to, src, mv, rs, ok, b):
                for t in range(TT):
                    eng.tensor_scalar(to[:, t, :], src[:, t, :], mv[:, t, 0:1], rs[:, t:t + 1],
                                      ALU.subtract, ALU.mult).then_inc(ok.sem, 1)

            def epsilon(ve, mv, ok, mv_ok, read, b):
                if b.past(1):
                    eng.wait_ge(read.sem, read.at(b.ago(1)))
                eng.wait_ge(mv_ok.sem, mv_ok.at(b))
                eng.tensor_scalar(ve[:, :], mv[:, :, 1], EPS, None, ALU.add).then_inc(ok.sem, 1)

            def slot(at):
                for h in range(HEADS):
                    b = at(0)
                    if b and h == 2:
                        max_low(b, 1)
                    b = at(1)
                    if b and h == 10:
                        max_low(b, 0)
                    b = at(-1)
                    if b:
                        if h in (4, 6):
                            t = (h - 4) // 2
                            tok = bank_c[:, :].rearrange("p (h c) -> p h c", h=HEADS)
                            eng.wait_ge(tok_up.sem, tok_up.at(b, t + 1))
                            if t == 0:
                                if b.past(1):
                                    eng.wait_ge(onT_up.sem, onT_up.at(b.ago(1)))
                            eng.reciprocal(r_sum[:, t, :], tok[:, :, DK]).then_inc(rs_ok.sem, 1)
                            eng.wait_ge(rs_ok.sem, rs_ok.at(b, t + 1))
                            eng.tensor_tensor(on[:, t, :, :], tok[:, :, 0:DK],
                                              r_sum[:, t, :].rearrange("p (h o) -> p h o", o=1)
                                              .broadcast_to([P, HEADS, DK]), ALU.mult).then_inc(on_ok.sem, 1)
                        if h == 12:
                            eng.wait_ge(att_up.sem, att_up.at(b))
                            eng.wait_ge(L3c_ok.sem, L3c_ok.at(b))
                            if b.past(2):
                                eng.wait_ge(n4_ok.sem, n4_ok.at(b.ago(2)))
                                eng.wait_ge(x12_ok.sem, x12_ok.at(b.ago(2)))
                            eng.tensor_tensor(x2[:, b.turnof(2), :, :].rearrange("p t d -> p (t d)"),
                                              bank_c[:, 0:TT * D],
                                              L3c[:, b.turnof(4), :, :].rearrange("p t d -> p (t d)"), ALU.add)\
                               .then_inc(x2_ok.sem, 1)
                    b = at(4)
                    if b:
                        k = b.turnof(2)
                        if h == 8:
                            eng.wait_ge(sg_ok.sem, sg_ok.at(b))
                            if b.past(1):
                                eng.wait_ge(o_up.sem, o_up.at(b.ago(1)))
                            for f in range(FB):
                                eng.scalar_tensor_tensor(gT[:, f, :], bank_a[:, f * N:(f + 1) * N], b_z[:, f:f + 1],
                                                         sg[:, f, :], ALU.add, ALU.mult).then_inc(gT_ok.sem, 1)
                        if h == 10:
                            eng.wait_ge(o_up.sem, o_up.at(b))
                            eng.wait_ge(Lb_ok.sem, Lb_ok.at(b))
                            if b.past(2):
                                eng.wait_ge(a_ok.sem, a_ok.at(b.ago(2)))
                            eng.tensor_tensor(r[:, k, :, :].rearrange("p t d -> p (t d)"), bank_a[:, 0:TT * D],
                                              Lb[:, :, :].rearrange("p t d -> p (t d)"), ALU.add)\
                               .then_inc(r_ok.sem, 1)
                    b = at(-3)
                    if b and h == 9:
                        eng.wait_ge(y_up.sem, y_up.at(b))
                        eng.wait_ge(x12_ok.sem, x12_ok.at(b))
                        if b.past(1):
                            eng.wait_ge(o_out.sem, o_out.at(b.ago(1)))
                        eng.tensor_tensor(ob[:, :, :].rearrange("p t d -> p (t d)"), bank_d[:, 0:TT * D],
                                          x12[:, b.turnof(4), :, :].rearrange("p t d -> p (t d)"), ALU.add)\
                           .then_inc(ob_ok.sem, 1)
                    b = at(-2)
                    if b and h == 3:
                        eng.wait_ge(gate_up.sem, gate_up.at(b))
                        if b.past(1):
                            eng.wait_ge(at_ok.sem, at_ok.at(b.ago(1)))
                        for t in range(TT):
                            ins = eng.tensor_tensor(gate[:, t, :], bank_d[:, t * GATE_COLS:t * GATE_COLS + E],
                                                    b_gate_r[:, :], ALU.add)
                        ins.then_inc(gate_ok.sem, 1)
                    b = at(1)
                    if b:
                        eng.wait_ge(m_up.sem, m_up.at(b, h + 1))
                        if h == 0:
                            if b.past(2):
                                eng.wait_ge(mT_up.sem, mT_up.at(b.ago(2)))
                        eng.tensor_reduce(neg_max[:, b.turnof(2), :, h],
                                          bank_m[h % 2][:, :].rearrange("p (t n) -> p t n", t=TT), AX_X, ALU.max,
                                          negate=True).then_inc(m_ok.sem, 1)
                    b = at(4)
                    if b:
                        k = b.turnof(2)
                        if h == 0:
                            eng.wait_ge(x_in[k].sem, x_in[k].at(b))
                            if b.past(1):
                                eng.wait_ge(ve1_ok.sem, ve1_ok.at(b.ago(1)))
                                eng.wait_ge(L_ok.sem, L_ok.at(b.ago(1)))
                            stats(xin[:, k], stats1, st1, mv1, mv1_ok, b)
                            epsilon(ve1, mv1, ve1_ok, mv1_ok, rstd1_ok, b)
                        if h == 2:
                            eng.wait_ge(rstd1_ok.sem, rstd1_ok.at(b))
                            if b.past(2):
                                eng.wait_ge(Lb_ok.sem, Lb_ok.at(b.ago(2)))
                                eng.wait_ge(LT_up.sem, LT_up.at(b.ago(2)))
                            centred(L[:, k], xin[:, k], mv1, rstd1, L_ok, b)
                    b = at(3)
                    if b:
                        k = b.turnof(2)
                        if h == 0:
                            eng.wait_ge(r_ok.sem, r_ok.at(b))
                            if b.past(1):
                                eng.wait_ge(ve2_ok.sem, ve2_ok.at(b.ago(1)))
                                eng.wait_ge(a_ok.sem, a_ok.at(b.ago(1)))
                            stats(r[:, k], stats2, st2, mv2, mv2_ok, b)
                            epsilon(ve2, mv2, ve2_ok, mv2_ok, rstd2_ok, b)
                        if h == 3:
                            eng.wait_ge(rstd2_ok.sem, rstd2_ok.at(b))
                            if b.past(1):
                                eng.wait_ge(x1_ok.sem, x1_ok.at(b.ago(1), 1))
                            centred(a, r[:, k], mv2, rstd2, a_ok, b)
                        if h == 6:
                            eng.wait_ge(x1_ok.sem, x1_ok.at(b))
                            if b.past(2):
                                eng.wait_ge(n3_ok.sem, n3_ok.at(b.ago(2)))
                                eng.wait_ge(L3_ok.sem, L3_ok.at(b.ago(2)))
                            stats(x1[:, k], stats3, st3, mv3[:, k], mv3_ok, b)
                            if b.past(1):
                                eng.wait_ge(rstd3_ok.sem, rstd3_ok.at(b.ago(1)))
                            eng.wait_ge(mv3_ok.sem, mv3_ok.at(b))
                            eng.tensor_scalar(ve3[:, 0, :], mv3[:, k, :, 1], EPS, None, ALU.add)\
                               .then_inc(ve3_ok.sem, 1)
                            eng.tensor_scalar(ve3[:, 1, :], mv3[:, k, :, 1], 1.0 + EPS, EPS * EPS, ALU.mult, ALU.add)\
                               .then_inc(ve3_ok.sem, 1)
                        if h == 9:
                            eng.wait_ge(rstd3_ok.sem, rstd3_ok.at(b))
                            if b.past(1):
                                eng.wait_ge(nT_up.sem, nT_up.at(b.ago(1)))
                            centred(n3, x1[:, k], mv3[:, k], rstd3[:, k, 1], n3_ok, b)
                    b = at(2)
                    if b and h == 5:
                        k = b.turnof(2)
                        eng.wait_ge(rstd3_ok.sem, rstd3_ok.at(b))
                        if b.past(1):
                            eng.wait_ge(L3c_ok.sem, L3c_ok.at(b.ago(1)))
                        centred(L3, x1[:, k], mv3[:, k], rstd3[:, k, 0], L3_ok, b)
                    b = at(-1)
                    if b:
                        if h == 12:
                            eng.wait_ge(x2_ok.sem, x2_ok.at(b))
                            if b.past(1):
                                eng.wait_ge(ve4_ok.sem, ve4_ok.at(b.ago(1)))
                                eng.wait_ge(n4_ok.sem, n4_ok.at(b.ago(1)))
                            stats(x2[:, b.turnof(2)], stats4, st4, mv4, mv4_ok, b)
                            epsilon(ve4, mv4, ve4_ok, mv4_ok, rstd4_ok, b)
                        if h == 14:
                            eng.wait_ge(rstd4_ok.sem, rstd4_ok.at(b))
                            if b.past(1):
                                eng.wait_ge(n4T_up.sem, n4T_up.at(b.ago(1)))
                            centred(n4, x2[:, b.turnof(2)], mv4, rstd4, n4_ok, b)
                    b = at(-2)
                    if b:
                        if h == 3:
                            eng.wait_ge(gate_ok.sem, gate_ok.at(b))
                            carry(eng, b)
                            for t in range(TT):
                                eng.max(top[:, t, :], gate[:, t, :]).then_inc(top_ok.sem, 1)
                        if h == 4:
                            for t in range(TT):
                                eng.wait_ge(top_ok.sem, top_ok.at(b, t + 1))
                                carry(eng, b)
                                eng.max_index(top_at[:, t, :], top[:, t, :], gate[:, t, :]).then_inc(at_ok.sem, 1)
                            if b.past(1):
                                eng.wait_ge(eg_ok.sem, eg_ok.at(b.ago(1)))
                            eng.tensor_tensor(gap[:, :], top[:, :, 1], top[:, :, 0], ALU.subtract)\
                               .then_inc(gap_ok.sem, 1)
                        if h == 7:
                            eng.wait_ge(at_ok.sem, at_ok.at(b))
                            if b.past(1):
                                eng.wait_ge(pick_ok.sem, pick_ok.at(b.ago(1)))
                            eng.tensor_copy(top_atf[:, :, :], top_at[:, :, :]).then_inc(atf_ok.sem, 1)
                        if h == 8:
                            eng.wait_ge(eg_ok.sem, eg_ok.at(b))
                            eng.tensor_scalar(denom[:, :], e_gap[:, :], 1.0, None, ALU.add).then_inc(den_ok.sem, 1)
                            eng.wait_ge(den_ok.sem, den_ok.at(b))
                            eng.reciprocal(prob2[:, 0, :], denom[:, :]).then_inc(p1_ok.sem, 1)
                        if h == 9:
                            eng.wait_ge(p1_ok.sem, p1_ok.at(b))
                            eng.tensor_tensor(prob2[:, 1, :], prob2[:, 0, :], e_gap[:, :], ALU.mult)\
                               .then_inc(p2_ok.sem, 1)
                        if h == 10:
                            eng.wait_ge(atf_ok.sem, atf_ok.at(b))
                            eng.wait_ge(p2_ok.sem, p2_ok.at(b))
                            if b.past(1):
                                eng.wait_ge(mw_ok.sem, mw_ok.at(b.ago(1)))
                            for t in range(TT):
                                for n in range(2):
                                    eng.tensor_scalar(pick[:, n, t, :], iota_e[:, :], top_atf[:, t, n:n + 1],
                                                      prob2[:, n, t:t + 1], ALU.is_equal, ALU.mult)\
                                       .then_inc(pick_ok.sem, 1)
                        if h == 11:
                            eng.wait_ge(pick_ok.sem, pick_ok.at(b))
                            if b.past(1):
                                eng.wait_ge(mwT_up.sem, mwT_up.at(b.ago(1)))
                            eng.tensor_tensor(mix_w[:, :, :], pick[:, 0, :, :], pick[:, 1, :, :], ALU.add)\
                               .then_inc(mw_ok.sem, 1)

            def max_low(b, half):
                eng.wait_ge(mhi_ok.sem, mhi_ok.at(b, half + 1))
                if b.past(1):
                    eng.wait_ge(shift_in[half][b.turnof(2) ^ 1].sem, shift_in[half][b.turnof(2) ^ 1].at(b.ago(1)))
                eng.tensor_tensor(max_lo[:, half, :], bank_c[0:HEADS // 2, 0:N], max_hi[:, half, :],
                                  ALU.subtract).then_inc(mlo_ok.sem, 1)

            slots(eng, slot)

        @block.tensor
        def _(eng):
            eng.wait_ge(s_load, 16 * LOADS)
            eng.wait_ge(s_const, 4)
            for j in range(FB):
                ins = eng.transpose(bank_a[:, j * P:(j + 1) * P], w_in[:, j * P:(j + 1) * P], ident[:, :])
            ins.then_inc(s_fold_p, 1)
            eng.wait_ge(s_fold_v, FOLD_READY)
            ins = eng.matmul(bank_d[:, 0:1], w_qkv[:, 2, :], b1_c[:, 0:1], start=True, stop=True)
            for f in range(FB):
                for j in range(FB):
                    ins = eng.matmul(bank_c[:, f:f + 1], w_g[:, j, f * P:(f + 1) * P], b_in_c[:, j:j + 1],
                                     start=(j == 0), stop=(j == FB - 1))
            for w in range(2):
                ins = eng.matmul(bank_c[:, FB + w:FB + w + 1], x1[:, 0, w, :], b1_c[:, 0:1], start=True, stop=True)
            for j in range(HB):
                ins = eng.matmul(bank_c[:, FB + 2 + j:FB + 3 + j],
                                 w_1[:, :, :].rearrange("p e h -> p (e h)")[:, j * P:(j + 1) * P],
                                 b2_c[:, 0:1], start=True, stop=True)
            ins.then_inc(s_fold_p, 1)
            eng.wait_ge(s_fold_v, FOLD_V_WIDE)
            for j in range(FB):
                ins = eng.matmul(bank_a[:, 0:DIN], w_inT[:, j, :], w_g[:, j, :], start=(j == 0), stop=(j == FB - 1))
            ins = eng.matmul(bank_s[0][:, 0:D], b_v_wide[:, :], w_o[:, :], start=True, stop=True)
            ins = eng.matmul(bank_s[0][:, D:D + E], b2_wide[:, :], w_gate[:, :], start=True, stop=True)
            ins.then_inc(s_fold_p, 1)
            eng.wait_ge(s_fold_v, FOLD_V)

            def slot(at):
                for h in range(HEADS):
                    b = at(0)
                    if b:
                        k = b.turnof(4)
                        if h % (HEADS // 2) == 0:
                            eng.wait_ge(shift_in[h // (HEADS // 2)][b.turnof(2)].sem, shift_in[h // (HEADS // 2)][b.turnof(2)].at(b))
                        if b.past(1) or h - 1 > 0:
                            eng.wait_ge(p_ok.sem, p_ok.at(b, h - 1))
                        for t in range(TT):
                            ins = eng.matmul(bank_s[h % 2][:, t * N:(t + 1) * N],
                                             k_stack[k][:, h, t * P:(t + 1) * P], q_stack[k][:, h, :],
                                             start=True, stop=True)
                        ins.then_inc(s_up.sem, 1)
                    b = at(1)
                    if b:
                        k = b.turnof(4)
                        if h == 0:
                            eng.wait_ge(stacked[b.turnof(2)].sem, stacked[b.turnof(2)].at(b))
                            if b.turn is None and b.offset == 0:
                                eng.wait_ge(s_zero, SET_POOL)
                                eng.wait_ge(s_set, SET_VECTOR)
                        if b.past(1) or h - 1 > 0:
                            eng.wait_ge(m_ok.sem, m_ok.at(b, h - 1))
                        for t in range(TT):
                            ins = eng.matmul(bank_m[h % 2][:, t * N:(t + 1) * N],
                                             q_stack[k][0:SHIFT_ROW, h, t * P:(t + 1) * P],
                                             k_stack[k][0:SHIFT_ROW, h, :], start=True, stop=True)
                        ins.then_inc(m_up.sem, 1)
                    b = at(0)
                    if b:
                        if h == 1:
                            turn_max(b, 1)
                        if h % GROUP == 2 and h > GROUP:
                            weigh(b, h // GROUP - 1)
                    b = at(-1)
                    if b:
                        if h == 1:
                            weigh(b, GROUPS - 1)
                        if h in (3, 5):
                            t = (h - 3) // 2
                            eng.wait_ge(oT_ok.sem, oT_ok.at(b))
                            if t == 0:
                                if at(0):
                                    eng.wait_ge(mlo_ok.sem, mlo_ok.at(b.ago(-1)))
                                else:
                                    if b.past(1):
                                        eng.wait_ge(x2_ok.sem, x2_ok.at(b.ago(1)))
                            else:
                                eng.wait_ge(on_ok.sem, on_ok.at(b, 1))
                            for g in range(GROUPS):
                                ins = eng.transpose(bank_c[:, g * P:(g + 1) * P], oT[:, g, t * P:(t + 1) * P],
                                                    ident[:, :])
                            ins.then_inc(tok_up.sem, 1)
                        if h == 7:
                            eng.wait_ge(on_ok.sem, on_ok.at(b))
                            for t in range(TT):
                                ins = eng.transpose(bank_c[:, t * P:(t + 1) * P],
                                                    on[:, t, :, :].rearrange("p h d -> p (h d)"), ident[:, :])
                            ins.then_inc(onT_up.sem, 1)
                    b = at(1)
                    if b and h == 9:
                        turn_max(b, 0)
                    b = at(-1)
                    if b and h == 11:
                        eng.wait_ge(onT_ok.sem, onT_ok.at(b))
                        if at(1):
                            eng.wait_ge(mlo_ok.sem, mlo_ok.at(b.ago(-2), 1))
                        for t in range(TT):
                            ins = eng.matmul(bank_c[:, t * D:(t + 1) * D], onT[:, t * P:(t + 1) * P], w_o[:, :],
                                             start=True, stop=True)
                        ins.then_inc(att_up.sem, 1)
                    b = at(4)
                    if b:
                        k = b.turnof(2)
                        if h == 3:
                            eng.wait_ge(L_ok.sem, L_ok.at(b))
                            LT_free(b, at)
                            for t in range(TT):
                                ins = eng.transpose(bank_a[:, t * P:(t + 1) * P], L[:, k, t, :], ident[:, :])
                            ins.then_inc(LT_up.sem, 1)
                        if h == 5:
                            eng.wait_ge(LT_ok.sem, LT_ok.at(b))
                            for f in range(FB):
                                ins = eng.matmul(bank_a[:, f * N:(f + 1) * N], w_z[:, f * P:(f + 1) * P], LT[:, :],
                                                 start=True, stop=True)
                            ins.then_inc(z_up.sem, 1)
                        if h == 9:
                            eng.wait_ge(gT_ok.sem, gT_ok.at(b))
                            for t in range(TT):
                                for f in range(FB):
                                    ins = eng.matmul(bank_a[:, t * D:(t + 1) * D], gT[:, f, t * P:(t + 1) * P],
                                                     w_outs[:, f, :], start=(f == 0), stop=(f == FB - 1))
                            ins.then_inc(o_up.sem, 1)
                    b = at(3)
                    if b:
                        if h == 11:
                            eng.wait_ge(n3_ok.sem, n3_ok.at(b))
                            if at(4):
                                eng.wait_ge(r_ok.sem, r_ok.at(b.ago(-1)))
                            else:
                                if b.past(1):
                                    eng.wait_ge(v_ok.sem, v_ok.at(b.ago(1)))
                            for t in range(TT):
                                ins = eng.transpose(bank_a[:, t * P:(t + 1) * P], n3[:, t, :], ident[:, :])
                            ins.then_inc(nT_up.sem, 1)
                        if h == 13:
                            eng.wait_ge(nT_ok.sem, nT_ok.at(b))
                            for w in range(2):
                                ins = eng.matmul(bank_a[:, w * N:(w + 1) * N], w_qkvs[:, w, :], nT[:, :],
                                                 start=True, stop=True)
                            ins.then_inc(qk_up.sem, 1)
                        if h == 15:
                            eng.wait_ge(qk_ok.sem, qk_ok.at(b))
                            for t in range(TT):
                                ins = eng.matmul(bank_a[:, t * D:(t + 1) * D], nT[:, t * P:(t + 1) * P],
                                                 w_qkvs[:, 2, :], start=True, stop=True)
                            ins.then_inc(v_up.sem, 1)
                    b = at(-2)
                    if b:
                        k = b.turnof(2)
                        if h == 0:
                            eng.wait_ge(n4_ok.sem, n4_ok.at(b))
                            if b.past(1):
                                eng.wait_ge(mwT_ok.sem, mwT_ok.at(b.ago(1)))
                            for t in range(TT):
                                ins = eng.transpose(bank_d[:, t * P:(t + 1) * P], n4[:, t, :], ident[:, :])
                            ins.then_inc(n4T_up.sem, 1)
                        if h == 2:
                            eng.wait_ge(n4T_ok.sem, n4T_ok.at(b))
                            for t in range(TT):
                                ins = eng.matmul(bank_d[:, t * GATE_COLS:(t + 1) * GATE_COLS],
                                                 n4T[:, k, t * P:(t + 1) * P], w_gates[:, :], start=True, stop=True)
                            ins.then_inc(gate_up.sem, 1)
                    b = at(-2)
                    if b:
                        if h in (4, 6):
                            j0 = h - 4
                            if j0:
                                eng.wait_ge(h_ok.sem, h_ok.at(b, 2))
                            else:
                                eng.wait_ge(gate_ok.sem, gate_ok.at(b))
                            for j in (j0, j0 + 1):
                                ins = eng.matmul(bank_d[:, (j - j0) * N:(j - j0 + 1) * N],
                                                 w_1s[:, j * P:(j + 1) * P], n4T[:, b.turnof(2), :],
                                                 start=True, stop=True)
                            ins.then_inc(h_up.sem, 1)
                    b = at(-3)
                    if b and h == 8:
                        eng.wait_ge(hw_ok.sem, hw_ok.at(b))
                        if at(-2):
                            eng.wait_ge(h_ok.sem, h_ok.at(b.ago(-1)))
                        else:
                            eng.wait_ge(mwT_ok.sem, mwT_ok.at(b))
                        for t in range(TT):
                            for j in range(HB):
                                ins = eng.matmul(bank_d[:, t * D:(t + 1) * D], hidw[:, j, t * P:(t + 1) * P],
                                                 w_2[:, j, :], start=(j == 0), stop=(j == HB - 1))
                        ins.then_inc(y_up.sem, 1)
                    b = at(-2)
                    if b:
                        if h == 12:
                            eng.wait_ge(mw_ok.sem, mw_ok.at(b))
                            if b.past(1):
                                eng.wait_ge(ob_ok.sem, ob_ok.at(b.ago(1)))
                            else:
                                eng.wait_ge(h_ok.sem, h_ok.at(b))
                            for t in range(TT):
                                ins = eng.transpose(bank_d[0:E, t * P:(t + 1) * P], mix_w[:, t, :], ident[:, :])
                            ins.then_inc(mwT_up.sem, 1)

            def LT_free(b, at):
                if b.past(2):
                    eng.wait_ge(v_ok.sem, v_ok.at(b.ago(2)))
                elif b.past(1):
                    eng.wait_ge(r_ok.sem, r_ok.at(b.ago(1)))

            def turn_max(b, half):
                eng.wait_ge(m_ok.sem, m_ok.at(b, (half + 1) * (HEADS // 2)))
                if half == 0:
                    if b.past(2):
                        eng.wait_ge(onT_ok.sem, onT_ok.at(b.ago(2)))
                    elif b.past(1):
                        eng.wait_ge(mlo_ok.sem, mlo_ok.at(b.ago(1)))
                else:
                    if b.past(2):
                        eng.wait_ge(x2_ok.sem, x2_ok.at(b.ago(2)))
                    eng.wait_ge(mlo_ok.sem, mlo_ok.at(b, 1))
                k = b.turnof(2)
                hs = slice(half * (HEADS // 2), (half + 1) * (HEADS // 2))
                for t in range(TT):
                    ins = eng.transpose(bank_c[0:HEADS // 2, t * P:(t + 1) * P], neg_max[:, k, t, hs], ident[:, :])
                ins.then_inc(mT_up.sem, 1)

            def weigh(b, g):
                k = b.turnof(4)
                eng.wait_ge(p_ok.sem, p_ok.at(b, GROUP * (g + 1)))
                eng.wait_ge(v_ok.sem, v_ok.at(b))
                if g % 2 == 0:
                    if b.past(1) or g // 2 > 0:
                        eng.wait_ge(oT_ok.sem, oT_ok.at(b, g // 2))
                for t in range(TT):
                    for j in range(GROUP):
                        h = GROUP * g + j
                        ins = eng.matmul(bank_o[32 * j:32 * (j + 1), (g % 2) * N:(g % 2 + 1) * N],
                                         v_one[:, k, t, h, :], probs[:, h % P_RING, t, :],
                                         start=(t == 0), stop=(t == TT - 1))
                ins.then_inc(pv_up.sem, 1)

            slots(eng, slot)


LOADS = 20
FOLD_READY = 11
FOLD_V_WIDE = 14
FOLD_V = 22
VECTOR_SETS = (0, 1)
POOL_SETS = (2, 3)
SET_VECTOR = len(VECTOR_SETS)
SET_POOL = 3 + len(POOL_SETS)


_INS = ["L0_attn_x", "L0_attn_W_in", "L0_attn_b_in", "L0_attn_b_sp", "L0_attn_W_g", "L0_attn_b_g", "L0_attn_W_out",
        "L0_attn_b_out", "L0_attn_norm_w", "L0_attn_norm_b", "L0_ffn_Wq", "L0_ffn_Wk", "L0_ffn_Wv", "L0_ffn_Wo",
        "L0_ffn_g1", "L0_ffn_b1", "L0_ffn_g2", "L0_ffn_b2", "L0_ffn_Wg", "L0_ffn_W1", "L0_ffn_W2"]


def kernel(**inputs):
    import numpy as _np
    import concourse.bacc as _bacc
    from concourse import mybir as _mybir
    from concourse.bass_utils import run_bass_kernel_spmd as _run

    nc = _bacc.Bacc("TRN2", target_bir_lowering=False, num_devices=1)
    arrays, args = {}, []
    for name in _INS:
        v = _np.ascontiguousarray(inputs[name])
        arrays[f"in_{name}_dram"] = v
        args.append(nc.dram_tensor(f"in_{name}_dram", v.shape, _mybir.dt.from_np(v.dtype), kind="ExternalInput").ap())
    shape = inputs["L0_attn_x"].shape
    args.append(nc.dram_tensor("out_0_dram", shape, _mybir.dt.float32, kind="ExternalOutput").ap())
    build(nc, *args)
    got = _run(nc, [arrays], core_ids=[0])
    return got.results[0]["out_0_dram"]
```

```python
from contextlib import ExitStack

import concourse.bass as bass
from concourse import mybir

F32 = mybir.dt.float32
BF16 = mybir.dt.bfloat16
U32 = mybir.dt.uint32
ALU = mybir.AluOpType
ACT = mybir.ActivationFunctionType
AX_X = mybir.AxisListType.X
EPS = 1e-5

P = 128
HEADS = 16
GROUP = 4
GROUPS = HEADS // GROUP
ORDER = [8 * u + 2 * j + o for u in range(HEADS // 8) for o in range(2) for j in range(GROUP)]
SPAN = 16
TERMS = ((0, 0), (0, 1), (1, 0), (0, 2), (2, 0), (1, 1))
PART_ROW = 32
SHIFT_ROW = PART_ROW + 8 * len(TERMS)
STACK_ROWS = SHIFT_ROW + 2
UNROLL = 4
WEIGH_AT = (7, 10, 12)
P_RING = 8
GATE_COLS = 96


class Batch:

    def __init__(self, turn, offset):
        self.turn, self.offset = turn, offset

    def ago(self, n):
        return Batch(self.turn, self.offset - n)

    def past(self, n):
        return self.turn is not None or self.offset >= n

    def turnof(self, n):
        return self.offset % n

    def index(self):
        return self.offset if self.turn is None else self.turn * UNROLL + self.offset


class Count:

    def __init__(self, sem, per, every=1):
        self.sem, self.per, self.every = sem, per, every

    def at(self, b, n=None):
        value = self.per * (b.offset // self.every) + (self.per if n is None else n)
        assert value > 0
        if b.turn is None:
            return value
        return b.turn * (self.per * (UNROLL // self.every)) + value


def build(nc, x, W_in, b_in, W_sp_bias, W_g, b_g, W_out, b_out, norm_w, norm_b,
          Wq, Wk, Wv, Wo, g1, b1, g2, b2, Wgate, W1, W2, out):
    B, T, D = x.shape
    TT = T // P
    DIN = W_in.shape[1]
    FB = DIN // P
    DK = D // HEADS
    E, _, EH = W1.shape
    HB = E * EH // P
    EPB = P // EH
    N = T
    assert D == P and TT == 2 and DIN == 2 * P and DK == 8 and EPB == 2 and E == 8
    SCALE = float(DK) ** -0.5

    with ExitStack() as ctx:
        def sb(name, shape, dt=F32):
            return ctx.enter_context(nc.sbuf_tensor(name, shape, dt))

        def bank(name):
            return ctx.enter_context(nc.psum_tensor(name, [P, 512], F32))

        def sem(name):
            return ctx.enter_context(nc.semaphore(name))

        def count(name, per, every=1):
            if every == 1:
                return Count(sem(name), per)
            return [Count(sem(f"{name}{k}"), per, every) for k in range(every)]

        ident = sb("ident", [P, P])
        minus_half = sb("minus_half", [P, 2 * TT])
        iota_e = sb("iota_e", [P, E])
        w_in = sb("w_in", [P, DIN])
        w_inT = sb("w_inT", [P, FB, P])
        w_g = sb("w_g", [P, FB, DIN])
        b_in_c = sb("b_in_c", [P, FB])
        b_g_c = sb("b_g_c", [P, FB])
        b_sp_c = sb("b_sp_c", [P, FB])
        w_z = sb("w_z", [P, DIN])
        b_z = sb("b_z", [P, FB])
        b_z_half = sb("b_z_half", [P, FB])
        w_out = sb("w_out", [P, FB, D])
        w_outs = sb("w_outs", [P, FB, D])
        b_out_r = sb("b_out_r", [P, D])
        norm_w_r = sb("norm_w_r", [P, D])
        norm_b_r = sb("norm_b_r", [P, D])
        w_qkv = sb("w_qkv", [P, 3, D])
        w_qkvs = sb("w_qkvs", [P, 3, D])
        w_o = sb("w_o", [P, D])
        g1_c = sb("g1_c", [P, 1])
        b1_c = sb("b1_c", [P, 1])
        g2_c = sb("g2_c", [P, 1])
        b2_c = sb("b2_c", [P, 1])
        b_qk = sb("b_qk", [P, 2])
        b_v = sb("b_v", [P, 1])
        ones = sb("ones", [P, P])
        b_v_wide = sb("b_v_wide", [P, P])
        b2_wide = sb("b2_wide", [P, P])
        c_row = sb("c_row", [P, D])
        w_gate = sb("w_gate", [P, E])
        w_gates = sb("w_gates", [P, GATE_COLS])
        b_gate_r = sb("b_gate_r", [P, E])
        w_1 = sb("w_1", [P, E, EH])
        w_1s = sb("w_1s", [P, E * EH])
        b_1 = sb("b_1", [P, HB])
        w_2 = sb("w_2", [P, HB, D])

        xin = sb("xin", [P, 2, TT, D])
        stats1 = sb("stats1", [P, TT, 6])
        mv1 = sb("mv1", [P, TT, 2])
        ve1 = sb("ve1", [P, TT])
        rstd1 = sb("rstd1", [P, TT])
        L = sb("L", [P, 2, TT, D])
        Lb = sb("Lb", [P, TT, D])
        xb = sb("xb", [P, 2, TT, D])
        LT = sb("LT", [P, N])
        th = sb("th", [P, FB, N])
        sg = sb("sg", [P, FB, N])
        gT = sb("gT", [P, FB, N])
        r = sb("r", [P, 2, TT, D])
        stats2 = sb("stats2", [P, TT, 6])
        mv2 = sb("mv2", [P, TT, 2])
        ve2 = sb("ve2", [P, TT])
        rstd2 = sb("rstd2", [P, TT])
        a = sb("a", [P, TT, D])
        aw = sb("aw", [P, TT, D])
        x1 = sb("x1", [P, 2, TT, D])
        x1_kept = sb("x1_kept", [P, 4, TT, D])
        stats3 = sb("stats3", [P, TT, 6])
        mv3 = sb("mv3", [P, 2, TT, 2])
        ve3 = sb("ve3", [P, 2, TT])
        rstd3 = sb("rstd3", [P, 2, 2, TT])
        shift3 = sb("shift3", [P, 2, TT])
        n3 = sb("n3", [P, TT, D])
        L3 = sb("L3", [P, TT, D])
        L3c = sb("L3c", [P, 4, TT, D])
        nT = sb("nT", [P, N])
        qk = sb("qk", [P, 2, N])
        rest = sb("rest", [P, 2, N])
        parts = sb("parts", [P, 3, 2, N], BF16)
        q_stack = [sb(f"q_stack{k}", [STACK_ROWS, HEADS, N], BF16) for k in range(4)]
        k_stack = [sb(f"k_stack{k}", [STACK_ROWS, HEADS, N], BF16) for k in range(4)]
        v_one = sb("v_one", [P, 4, TT, HEADS, 32])
        neg_max = sb("neg_max", [P, 2, HEADS, TT])
        max_hi = sb("max_hi", [HEADS // 2 * TT, 2, P], BF16)
        max_lo = sb("max_lo", [HEADS // 2 * TT, 2, P], BF16)
        probs = sb("probs", [P, P_RING, TT, N])
        oT = sb("oT", [P, 2, N])
        r_sum = sb("r_sum", [P, TT, HEADS])
        on = sb("on", [P, TT, HEADS, DK])
        onT = sb("onT", [P, N])
        x2 = sb("x2", [P, 2, TT, D])
        x12 = sb("x12", [P, 4, TT, D])
        stats4 = sb("stats4", [P, TT, 6])
        mv4 = sb("mv4", [P, TT, 2])
        ve4 = sb("ve4", [P, TT])
        rstd4 = sb("rstd4", [P, TT])
        n4 = sb("n4", [P, TT, D])
        n4T = sb("n4T", [P, 2, N])
        gate = sb("gate", [P, TT, E])
        top = sb("top", [P, TT, 8])
        top_at = sb("top_at", [P, TT, 8], U32)
        top_atf = sb("top_atf", [P, TT, 8])
        gap = sb("gap", [P, TT])
        e_gap = sb("e_gap", [P, TT])
        denom = sb("denom", [P, TT])
        prob2 = sb("prob2", [P, 2, TT])
        pick = sb("pick", [P, 2, TT, E])
        mix_w = sb("mix_w", [P, E, TT])
        mix_wT = sb("mix_wT", [E * TT, P])
        mix_wide = sb("mix_wide", [P, HB, N])
        hid = sb("hid", [P, 2, HB, N])
        hidw = sb("hidw", [P, HB, N])
        ob = sb("ob", [P, TT, D])
        mix_dram = nc.dram_tensor("mix_dram", [E, N], F32, kind="Internal").ap()

        bank_s = [bank(f"bank_s{k}") for k in range(2)]
        bank_m = [bank(f"bank_m{k}") for k in range(2)]
        bank_o = bank("bank_o")
        bank_a = bank("bank_a")
        bank_c = bank("bank_c")
        bank_d = bank("bank_d")

        carrier = sem("carrier")
        s_load_z = sem("s_load_z")
        s_load_mix = sem("s_load_mix")
        s_load = sem("s_load")
        s_const = sem("s_const")
        s_zero = sem("s_zero")
        s_set = sem("s_set")
        s_copied = sem("s_copied")
        s_fold_v = sem("s_fold_v")
        s_fold_p = sem("s_fold_p")
        x_in = count("x_in", 16, 2)
        st1 = count("st1", TT)
        mv1_ok = count("mv1_ok", TT)
        ve1_ok = count("ve1_ok", 1)
        rstd1_ok = count("rstd1_ok", 1)
        L_ok = count("L_ok", TT)
        Lb_ok = count("Lb_ok", 1)
        xb_ok = count("xb_ok", 1)
        LT_up = count("LT_up", 1)
        LT_ok = count("LT_ok", 1)
        z_up = count("z_up", 1)
        th_ok = count("th_ok", FB)
        sg_ok = count("sg_ok", FB)
        gT_ok = count("gT_ok", FB)
        o_up = count("o_up", 1)
        r_ok = count("r_ok", 1)
        st2 = count("st2", TT)
        mv2_ok = count("mv2_ok", TT)
        ve2_ok = count("ve2_ok", 1)
        rstd2_ok = count("rstd2_ok", 1)
        a_ok = count("a_ok", TT)
        x1_ok = count("x1_ok", 2)
        st3 = count("st3", TT)
        mv3_ok = count("mv3_ok", TT)
        ve3_ok = count("ve3_ok", 2)
        rstd3_ok = count("rstd3_ok", 1)
        shift3_ok = count("shift3_ok", 1)
        n3_ok = count("n3_ok", TT)
        L3_ok = count("L3_ok", TT)
        kept = count("kept", 1)
        L3c_ok = count("L3c_ok", 1)
        nT_up = count("nT_up", 1)
        nT_ok = count("nT_ok", 1)
        qk_up = count("qk_up", 1)
        qk_ok = count("qk_ok", 2)
        v_up = count("v_up", 1)
        v_ok = count("v_ok", 1)
        hi_ok = count("hi_ok", 1)
        rest_ok = count("rest_ok", 1)
        mid_ok = count("mid_ok", 1)
        low_ok = count("low_ok", 1)
        stacked = count("stacked", 16 * 2 * len(TERMS), 2)
        m_up = count("m_up", HEADS)
        m_ok = count("m_ok", HEADS)
        mT_up = count("mT_up", 2)
        mhi_ok = count("mhi_ok", 2)
        mlo_ok = count("mlo_ok", 2)
        shift_in = [count(f"shift_in{half}_", 32, 2) for half in range(2)]
        s_up = count("s_up", HEADS)
        p_ok = count("p_ok", HEADS)
        pv_up = count("pv_up", GROUPS)
        oT_ok = count("oT_ok", 2)
        tok_up = count("tok_up", 1)
        rs_ok = count("rs_ok", 1)
        on_ok = count("on_ok", 1)
        onT_up = count("onT_up", 1)
        onT_ok = count("onT_ok", 1)
        att_up = count("att_up", 1)
        x2_ok = count("x2_ok", 1)
        x12_ok = count("x12_ok", 1)
        st4 = count("st4", TT)
        mv4_ok = count("mv4_ok", TT)
        ve4_ok = count("ve4_ok", 1)
        rstd4_ok = count("rstd4_ok", 1)
        n4_ok = count("n4_ok", TT)
        n4T_up = count("n4T_up", 1)
        n4T_ok = count("n4T_ok", 1)
        gate_up = count("gate_up", 1)
        gate_ok = count("gate_ok", 1)
        top_ok = count("top_ok", TT)
        at_ok = count("at_ok", TT)
        atf_ok = count("atf_ok", 1)
        gap_ok = count("gap_ok", 1)
        eg_ok = count("eg_ok", 1)
        den_ok = count("den_ok", 1)
        p1_ok = count("p1_ok", 1)
        p2_ok = count("p2_ok", 1)
        pick_ok = count("pick_ok", 2 * TT)
        mw_ok = count("mw_ok", 1)
        mwT_up = count("mwT_up", 1)
        mwT_ok = count("mwT_ok", 1)
        mw_out = count("mw_out", 16)
        mw_wide = count("mw_wide", 32)
        h_up = count("h_up", HB // 2)
        h_ok = count("h_ok", HB)
        hw_ok = count("hw_ok", TT)
        y_up = count("y_up", TT)
        ob_ok = count("ob_ok", 1)
        o_out = count("o_out", 16)

        FIRST, LOOP0 = -4, 4
        TURNS = (B - 4 - LOOP0) // UNROLL
        AFTER = LOOP0 + UNROLL * TURNS
        LAST = B + 3

        def slots(eng, slot):
            def batches(s, turn=None):
                def at(ahead):
                    b = s + ahead
                    return Batch(turn, b) if turn is not None or 0 <= b < B else None
                return at

            for s in range(FIRST, LOOP0):
                slot(batches(s))
            with eng.Fori(0, TURNS) as turn:
                for u in range(UNROLL):
                    slot(batches(LOOP0 + u, turn))
            for s in range(AFTER, LAST):
                slot(batches(s))

        def carry(eng, b):
            if b.turn is not None:
                eng.sem_inc(carrier, 1)

        def v_places(k):
            two = v_one[:, k, :, :, :].rearrange("p t h c -> p (t h c)").rearrange("p (u q c) -> p u q c", q=4, c=SPAN)
            return two[:, :, 0:4:3, :]

        block = ctx.enter_context(nc.Block())

        @block.sync
        def _(eng):
            def row(v):
                return v.rearrange("(o n) -> o n", o=1).broadcast_to([P, v.shape[0]])

            def cols(v):
                return v.rearrange("(c p) -> p c", p=P)

            def slot(at):
                b = at(0)
                if b:
                    shift(b, 0)
                b = at(4)
                if b and b.past(2):
                    load_x(b)
                b = at(1)
                if b:
                    eng.wait_ge(low_ok.sem, low_ok.at(b))
                    carry(eng, b)
                    stack_up(b, 2)
                b = at(-3)
                if b:
                    eng.wait_ge(mwT_ok.sem, mwT_ok.at(b))
                    carry(eng, b)
                    if b.past(1):
                        eng.wait_ge(mw_wide.sem, mw_wide.at(b.ago(1)))
                        carry(eng, b)
                    eng.dma_start(mix_dram.rearrange("e (t n) -> (e t) n", t=TT), mix_wT[:, :]).then_inc(mw_out.sem, 16)
                    eng.wait_ge(mw_out.sem, mw_out.at(b))
                    carry(eng, b)
                    if b.past(1):
                        eng.wait_ge(hw_ok.sem, hw_ok.at(b.ago(1)))
                        carry(eng, b)
                    src = mix_dram.rearrange("(j o) n -> o j n", o=EPB)
                    for o in range(EPB):
                        eng.dma_start(mix_wide[o * EH:(o + 1) * EH, :, :],
                                      src[o:o + 1, :, :].broadcast_to([EH, HB, N])).then_inc(mw_wide.sem, 16)
                b = at(-4)
                if b:
                    store(b)
                b = at(0)
                if b:
                    shift(b, 1)
                b = at(2)
                if b:
                    if b.turn is None and b.offset == 0:
                        eng.wait_ge(s_copied, 16 * copies)
                    if b.past(4):
                        eng.wait_ge(s_up.sem, s_up.at(b.ago(4)))
                        carry(eng, b)
                        eng.wait_ge(m_up.sem, m_up.at(b.ago(4)))
                        carry(eng, b)
                    eng.wait_ge(hi_ok.sem, hi_ok.at(b))
                    carry(eng, b)
                    stack_up(b, 0)
                    eng.wait_ge(mid_ok.sem, mid_ok.at(b))
                    carry(eng, b)
                    stack_up(b, 1)

            def store(b):
                eng.wait_ge(ob_ok.sem, ob_ok.at(b))
                carry(eng, b)
                eng.dma_start(out[b.index(), :, :].rearrange("(t p) d -> p t d", p=P), ob[:, :, :])\
                   .then_inc(o_out.sem, 16)

            def load_x(b):
                k = b.turnof(2)
                if b.past(2):
                    eng.wait_ge(xb_ok.sem, xb_ok.at(b.ago(2)))
                    carry(eng, b)
                    eng.wait_ge(L_ok.sem, L_ok.at(b.ago(2)))
                    carry(eng, b)
                eng.dma_start(xin[:, k, :, :], x[b.index(), :, :].rearrange("(t p) d -> p t d", p=P))\
                   .then_inc(x_in[k].sem, 16)

            def stack_up(b, part):
                for t, pair in enumerate(TERMS):
                    for which, stack in enumerate((q_stack[b.turnof(4)], k_stack[b.turnof(4)])):
                        if pair[which] == part:
                            row = PART_ROW + DK * t
                            eng.dma_start(stack[row:row + DK, :, :], parts[:, part, which, :])\
                               .then_inc(stacked[b.turnof(2)].sem, 16)

            def shift(b, half):
                k4, k2 = b.turnof(4), b.turnof(2)
                eng.wait_ge(mlo_ok.sem, mlo_ok.at(b, half + 1))
                carry(eng, b)
                eng.wait_ge(mhi_ok.sem, mhi_ok.at(b, half + 1))
                carry(eng, b)
                if b.past(4):
                    eng.wait_ge(s_up.sem, s_up.at(b.ago(4)))
                    carry(eng, b)
                hs = slice(half * (HEADS // 2), (half + 1) * (HEADS // 2))
                eng.dma_start(q_stack[k4][SHIFT_ROW:SHIFT_ROW + 1, hs, :], max_hi[:, half, :])\
                   .then_inc(shift_in[half][k2].sem, 16)
                eng.dma_start(q_stack[k4][SHIFT_ROW + 1:SHIFT_ROW + 2, hs, :], max_lo[:, half, :])\
                   .then_inc(shift_in[half][k2].sem, 16)

            z_loads = [
                (w_in[:, :], W_in), (w_g[:, :, :], W_g.rearrange("(j p) n -> p j n", p=P)), (b_in_c[:, :], cols(b_in)),
            ]
            mix_loads = [
                (b_g_c[:, :], cols(b_g)), (b_sp_c[:, :], cols(W_sp_bias)),
                (w_out[:, :, :], W_out.rearrange("(j p) n -> p j n", p=P)),
                (b_out_r[:, :], row(b_out)), (norm_w_r[:, :], row(norm_w)), (norm_b_r[:, :], row(norm_b)),
            ]
            loads = [
                (w_qkv[:, 0, :], Wq), (w_qkv[:, 1, :], Wk), (w_qkv[:, 2, :], Wv), (w_o[:, :], Wo),
                (g1_c[:, :], cols(g1)), (b1_c[:, :], cols(b1)), (g2_c[:, :], cols(g2)), (b2_c[:, :], cols(b2)),
                (w_gate[:, :], Wgate), (w_1[:, :, :], W1.rearrange("e d h -> d e h")),
                (w_2[:, :, :], W2.rearrange("(j o) h d -> (o h) j d", o=EPB)),
            ]
            assert (len(z_loads), len(mix_loads), len(loads)) == (Z_LOADS, MIX_LOADS, LOADS)
            for to, of in z_loads:
                eng.dma_start(to, of, allow_slow_non_contiguous=True).then_inc(s_load_z, 16)
            load_x(Batch(None, 0))
            for to, of in mix_loads:
                eng.dma_start(to, of, allow_slow_non_contiguous=True).then_inc(s_load_mix, 16)
            for to, of in loads:
                eng.dma_start(to, of, allow_slow_non_contiguous=True).then_inc(s_load, 16)
            load_x(Batch(None, 1))
            eng.wait_ge(s_set, 2)
            copies = 0
            for stack in k_stack + q_stack[1:]:
                eng.dma_start(stack[0:PART_ROW, :, :], q_stack[0][0:PART_ROW, :, :]).then_inc(s_copied, 16)
                copies += 1
            for stack in k_stack[1:]:
                eng.dma_start(stack[SHIFT_ROW:STACK_ROWS, :, :], k_stack[0][SHIFT_ROW:STACK_ROWS, :, :])\
                   .then_inc(s_copied, 16)
                copies += 1

            slots(eng, slot)
            store(Batch(None, B - 1))
            eng.wait_ge(o_out.sem, o_out.at(Batch(None, B - 1)))

        @block.gpsimd
        def _(eng):
            eng.memset(ident[:, :], 0.0).then_inc(s_zero, 1)
            eng.wait_ge(s_zero, 1)
            eng.affine_select(out=ident[:, :], in_=ident[:, :], compare_op=ALU.not_equal, fill=1.0, base=0,
                              pattern=[[-1, P]], channel_multiplier=1).then_inc(s_const, 1)
            eng.memset(minus_half[:, :], -0.5).then_inc(s_const, 1)
            eng.memset(ones[:, :], 1.0).then_inc(s_const, 1)
            eng.iota(iota_e[:, :], pattern=[[1, E]], base=0, channel_multiplier=0,
                     allow_small_or_imprecise_dtypes=True).then_inc(s_const, 1)
            eng.wait_ge(s_const, 4)
            eng.memset(v_one[:, :, :, :, :], 0.0).then_inc(s_zero, 1)
            eng.wait_ge(s_zero, 2)
            for k in range(4):
                eng.memset(v_places(k)[:, :, :, DK:DK + 1], 1.0).then_inc(s_zero, 1)
                eng.wait_ge(s_zero, 3 + k)
            assert SET_POOL == 6
            eng.wait_ge(s_load_mix, 16 * MIX_LOADS)

            def wide(v):
                return v[:, :].rearrange("p (o d) -> p o d", o=1).broadcast_to([P, TT, D])

            def slot(at):
                b = at(3)
                if b:
                    eng.wait_ge(ve2_ok.sem, ve2_ok.at(b))
                    if b.past(1):
                        eng.wait_ge(a_ok.sem, a_ok.at(b.ago(1)))
                    eng.tensor_tensor(rstd2[:, :], ve2[:, :], minus_half[:, 0:TT], ALU.pow).then_inc(rstd2_ok.sem, 1)
                    eng.wait_ge(rstd2_ok.sem, rstd2_ok.at(b))
                    if b.past(1):
                        eng.wait_ge(x1_ok.sem, x1_ok.at(b.ago(1), 1))
                    carry(eng, b)
                    for t in range(TT):
                        eng.tensor_scalar(a[:, t, :], r[:, b.turnof(2), t, :], mv2[:, t, 0:1], rstd2[:, t:t + 1],
                                          ALU.subtract, ALU.mult).then_inc(a_ok.sem, 1)
                b = at(4)
                if b:
                    eng.wait_ge(ve1_ok.sem, ve1_ok.at(b))
                    if b.past(1):
                        eng.wait_ge(L_ok.sem, L_ok.at(b.ago(1)))
                    eng.tensor_tensor(rstd1[:, :], ve1[:, :], minus_half[:, 0:TT], ALU.pow).then_inc(rstd1_ok.sem, 1)
                b = at(2)
                if b:
                    eng.wait_ge(hi_ok.sem, hi_ok.at(b))
                    if b.past(1):
                        eng.wait_ge(low_ok.sem, low_ok.at(b.ago(1)))
                        eng.wait_ge(mid_ok.sem, mid_ok.at(b.ago(1)))
                    eng.tensor_tensor(rest[:, :, :], qk[:, :, :], parts[:, 0, :, :], ALU.subtract)\
                       .then_inc(rest_ok.sem, 1)
                b = at(4)
                if b:
                    k = b.turnof(2)
                    if b.past(2):
                        eng.wait_ge(x1_ok.sem, x1_ok.at(b.ago(2)))
                    eng.wait_ge(x_in[k].sem, x_in[k].at(b))
                    eng.tensor_tensor(xb[:, k, :, :], xin[:, k, :, :], wide(norm_b_r), ALU.add)\
                       .then_inc(xb_ok.sem, 1)
                b = at(3)
                if b:
                    k = b.turnof(2)
                    eng.wait_ge(a_ok.sem, a_ok.at(b))
                    if b.past(1):
                        eng.wait_ge(x1_ok.sem, x1_ok.at(b.ago(1)))
                    eng.tensor_tensor(aw[:, :, :], a[:, :, :], wide(norm_w_r), ALU.mult).then_inc(x1_ok.sem, 1)
                    eng.wait_ge(x1_ok.sem, x1_ok.at(b, 1))
                    eng.wait_ge(xb_ok.sem, xb_ok.at(b))
                    if b.past(2):
                        eng.wait_ge(kept.sem, kept.at(b.ago(2)))
                        eng.wait_ge(L3_ok.sem, L3_ok.at(b.ago(2)))
                        eng.wait_ge(n3_ok.sem, n3_ok.at(b.ago(2)))
                    eng.tensor_tensor(x1[:, k, :, :], aw[:, :, :], xb[:, k, :, :], ALU.add)\
                       .then_inc(x1_ok.sem, 1)
                b = at(4)
                if b:
                    k = b.turnof(2)
                    eng.wait_ge(L_ok.sem, L_ok.at(b))
                    if b.past(1):
                        eng.wait_ge(r_ok.sem, r_ok.at(b.ago(1)))
                    eng.tensor_tensor(Lb[:, :, :], L[:, k, :, :], wide(b_out_r), ALU.add)\
                       .then_inc(Lb_ok.sem, 1)
                    if b.past(1):
                        eng.wait_ge(gT_ok.sem, gT_ok.at(b.ago(1)))
                    for f in range(FB):
                        eng.wait_ge(th_ok.sem, th_ok.at(b, f + 1))
                        carry(eng, b)
                        eng.tensor_scalar(sg[:, f, :], th[:, f, :], 0.5, 0.5, ALU.mult, ALU.add)\
                           .then_inc(sg_ok.sem, 1)
                b = at(3)
                if b:
                    k = b.turnof(2)
                    eng.wait_ge(ve3_ok.sem, ve3_ok.at(b))
                    if b.past(2):
                        eng.wait_ge(n3_ok.sem, n3_ok.at(b.ago(2)))
                        eng.wait_ge(L3_ok.sem, L3_ok.at(b.ago(2)))
                    eng.tensor_tensor(rstd3[:, k, :, :].rearrange("p k t -> p (k t)"),
                                      ve3[:, :, :].rearrange("p k t -> p (k t)"), minus_half[:, 0:2 * TT],
                                      ALU.pow).then_inc(rstd3_ok.sem, 1)
                b = at(2)
                if b:
                    eng.wait_ge(mid_ok.sem, mid_ok.at(b))
                    if b.past(1):
                        eng.wait_ge(stacked[b.ago(1).turnof(2)].sem, stacked[b.ago(1).turnof(2)].at(b.ago(1)))
                    eng.tensor_tensor(parts[:, 2, :, :], rest[:, :, :], parts[:, 1, :, :], ALU.subtract)\
                       .then_inc(low_ok.sem, 1)
                b = at(-3)
                if b:
                    eng.wait_ge(h_ok.sem, h_ok.at(b))
                    eng.wait_ge(mw_wide.sem, mw_wide.at(b))
                    if b.past(1):
                        eng.wait_ge(y_up.sem, y_up.at(b.ago(1)))
                    for t in range(TT):
                        ts = slice(t * P, (t + 1) * P)
                        eng.tensor_tensor(hidw[:, :, ts], hid[:, b.turnof(2), :, ts], mix_wide[:, :, ts], ALU.mult)\
                           .then_inc(hw_ok.sem, 1)
                b = at(2)
                if b:
                    k, k4 = b.turnof(2), b.turnof(4)
                    if b.turn is None and b.offset == 0:
                        eng.wait_ge(s_fold_v, FOLD_V)
                    eng.wait_ge(L3_ok.sem, L3_ok.at(b))
                    if b.past(4):
                        eng.wait_ge(x2_ok.sem, x2_ok.at(b.ago(4)))
                    eng.tensor_tensor(L3c[:, k4, :, :], L3[:, :, :], wide(c_row), ALU.add).then_inc(L3c_ok.sem, 1)
                b = at(-1)
                if b:
                    k4 = b.turnof(4)
                    eng.wait_ge(ve4_ok.sem, ve4_ok.at(b))
                    if b.past(1):
                        eng.wait_ge(n4_ok.sem, n4_ok.at(b.ago(1)))
                    eng.tensor_tensor(rstd4[:, :], ve4[:, :], minus_half[:, 0:TT], ALU.pow).then_inc(rstd4_ok.sem, 1)
                    eng.wait_ge(x2_ok.sem, x2_ok.at(b))
                    eng.wait_ge(kept.sem, kept.at(b))
                    if b.past(3):
                        eng.wait_ge(ob_ok.sem, ob_ok.at(b.ago(3)))
                    eng.tensor_tensor(x12[:, k4, :, :], x1_kept[:, k4, :, :], x2[:, b.turnof(2), :, :],
                                      ALU.add).then_inc(x12_ok.sem, 1)
            slots(eng, slot)

        @block.scalar
        def _(eng):
            def slot(at):
                for h in range(HEADS):
                    b = at(2)
                    if b and h == 0:
                        eng.wait_ge(v_up.sem, v_up.at(b))
                        if b.past(4):
                            eng.wait_ge(pv_up.sem, pv_up.at(b.ago(4)))
                        if b.turn is None and b.offset == 0:
                            eng.wait_ge(s_zero, SET_POOL)
                        eng.activation(v_places(b.turnof(4))[:, :, :, 0:DK],
                                       bank_c[:, 0:N].rearrange("p (u o d) -> p u o d", o=2, d=DK),
                                       ACT.Copy).then_inc(v_ok.sem, 1)
                    b = at(0)
                    if b and h == 2:
                        max_high(b, 1)
                    if b and h == 11:
                        turn_copy(b, 0)
                    b = at(1)
                    if b and h == 11:
                        max_high(b, 0)
                    b = at(-1)
                    if b and h == 2:
                        turn_copy(b, 1)
                    if b and h == 6:
                        eng.wait_ge(onT_up.sem, onT_up.at(b))
                        if b.past(1):
                            eng.wait_ge(att_up.sem, att_up.at(b.ago(1)))
                        eng.activation(onT[:, :], bank_c[:, 0:N], ACT.Copy).then_inc(onT_ok.sem, 1)
                    b = at(4)
                    if b and h == 4:
                        eng.wait_ge(LT_up.sem, LT_up.at(b))
                        if b.past(1):
                            eng.wait_ge(z_up.sem, z_up.at(b.ago(1)))
                        eng.activation(LT[:, :], bank_a[:, 0:N], ACT.Copy).then_inc(LT_ok.sem, 1)
                    if b and h == 6:
                        eng.wait_ge(z_up.sem, z_up.at(b))
                        if b.past(1):
                            eng.wait_ge(sg_ok.sem, sg_ok.at(b.ago(1)))
                        if b.turn is None and b.offset == 0:
                            eng.wait_ge(s_fold_v, FOLD_MIX)
                        for f in range(FB):
                            eng.activation(th[:, f, :], bank_a[:, f * N:(f + 1) * N], ACT.Tanh,
                                           bias=b_z_half[:, f:f + 1], scale=0.5).then_inc(th_ok.sem, 1)
                    b = at(-2)
                    if b and h == 13:
                        eng.wait_ge(mwT_up.sem, mwT_up.at(b))
                        if b.past(1):
                            eng.wait_ge(mw_out.sem, mw_out.at(b.ago(1)))
                        eng.activation(mix_wT[:, :], bank_d[0:E * TT, 0:P], ACT.Copy).then_inc(mwT_ok.sem, 1)
                    b = at(3)
                    if b and h == 12:
                        eng.wait_ge(nT_up.sem, nT_up.at(b))
                        if b.past(1):
                            eng.wait_ge(qk_up.sem, qk_up.at(b.ago(1)))
                            eng.wait_ge(v_up.sem, v_up.at(b.ago(1)))
                        eng.activation(nT[:, :], bank_a[:, 0:N], ACT.Copy).then_inc(nT_ok.sem, 1)
                    if b and h == 14:
                        eng.wait_ge(qk_up.sem, qk_up.at(b))
                        if b.turn is None and b.offset == 0:
                            eng.wait_ge(s_fold_v, FOLD_V)
                        if b.past(1):
                            eng.wait_ge(rest_ok.sem, rest_ok.at(b.ago(1)))
                            eng.wait_ge(hi_ok.sem, hi_ok.at(b.ago(1)))
                        for w in range(2):
                            eng.activation(qk[:, w, :], bank_a[:, w * N:(w + 1) * N], ACT.Identity,
                                           bias=b_qk[:, w:w + 1]).then_inc(qk_ok.sem, 1)
                    b = at(-2)
                    if b and h == 1:
                        eng.wait_ge(n4T_up.sem, n4T_up.at(b))
                        if b.past(2):
                            eng.wait_ge(h_up.sem, h_up.at(b.ago(2)))
                        eng.activation(n4T[:, b.turnof(2), :], bank_d[:, 0:N], ACT.Copy).then_inc(n4T_ok.sem, 1)
                    if b and h in (5, 7):
                        j0 = h - 5
                        eng.wait_ge(h_up.sem, h_up.at(b, j0 // 2 + 1))
                        if b.past(2):
                            eng.wait_ge(hw_ok.sem, hw_ok.at(b.ago(2)))
                        for j in (j0, j0 + 1):
                            eng.activation(hid[:, b.turnof(2), j, :],
                                           bank_d[:, (j - j0) * N:(j - j0 + 1) * N], ACT.Relu,
                                           bias=b_1[:, j:j + 1]).then_inc(h_ok.sem, 1)
                    b = at(0)
                    if b:
                        eng.wait_ge(s_up.sem, s_up.at(b, h + 1))
                        if b.past(1) or (h - P_RING) // GROUP + 1 > 0:
                            eng.wait_ge(pv_up.sem, pv_up.at(b, (h - P_RING) // GROUP + 1))
                        eng.activation(probs[:, h % P_RING, :, :], bank_s[h % 2][:, :], ACT.Exp)\
                           .then_inc(p_ok.sem, 1)
                    b = at(2)
                    if b and h == 9:
                        k = b.turnof(2)
                        eng.wait_ge(shift3_ok.sem, shift3_ok.at(b))
                        if b.past(1):
                            eng.wait_ge(L3c_ok.sem, L3c_ok.at(b.ago(1)))
                        for t in range(TT):
                            eng.activation(L3[:, t, :], x1[:, k, t, :], ACT.Identity, bias=shift3[:, k, t:t + 1],
                                           scale=rstd3[:, k, 0, t:t + 1]).then_inc(L3_ok.sem, 1)
                    if b and h == 8:
                        eng.wait_ge(x1_ok.sem, x1_ok.at(b))
                        if b.past(4):
                            eng.wait_ge(x12_ok.sem, x12_ok.at(b.ago(4)))
                        eng.activation(x1_kept[:, b.turnof(4), :, :], x1[:, b.turnof(2), :, :], ACT.Copy)\
                           .then_inc(kept.sem, 1)
                    if b and h == 5:
                        eng.wait_ge(rest_ok.sem, rest_ok.at(b))
                        eng.activation(parts[:, 1, :, :], rest[:, :, :], ACT.Copy).then_inc(mid_ok.sem, 1)
                    b = at(3)
                    if b and h == 15:
                        eng.wait_ge(qk_ok.sem, qk_ok.at(b))
                        if b.past(1):
                            eng.wait_ge(stacked[b.ago(1).turnof(2)].sem, stacked[b.ago(1).turnof(2)].at(b.ago(1)))
                        eng.activation(parts[:, 0, :, :], qk[:, :, :], ACT.Copy).then_inc(hi_ok.sem, 1)
                    b = at(-2)
                    if b and h == 5:
                        eng.wait_ge(gap_ok.sem, gap_ok.at(b))
                        if b.past(1):
                            eng.wait_ge(p2_ok.sem, p2_ok.at(b.ago(1)))
                        eng.activation(e_gap[:, :], gap[:, :], ACT.Exp).then_inc(eg_ok.sem, 1)

            def max_high(b, half):
                eng.wait_ge(mT_up.sem, mT_up.at(b, half + 1))
                if b.past(1):
                    eng.wait_ge(shift_in[half][b.turnof(2) ^ 1].sem, shift_in[half][b.turnof(2) ^ 1].at(b.ago(1)))
                eng.activation(max_hi[:, half, :], bank_c[0:HEADS // 2 * TT, 0:P], ACT.Copy).then_inc(mhi_ok.sem, 1)

            def turn_copy(b, u):
                eng.wait_ge(pv_up.sem, pv_up.at(b, 2 * u + 2))
                if b.past(1):
                    eng.wait_ge(tok_up.sem, tok_up.at(b.ago(1)))
                eng.activation(oT[:, u, :], bank_o[:, u * N:(u + 1) * N], ACT.Copy).then_inc(oT_ok.sem, 1)

            slots(eng, slot)

        @block.vector
        def _(eng):
            steps = [0]

            def folded(ins):
                steps[0] += 1
                ins.then_inc(s_fold_v, 1)

            eng.memset(q_stack[0][0:PART_ROW, :, :].bitcast(U32), 0).then_inc(s_set, 1)
            def fold_turned():
                eng.wait_ge(s_fold_p, 1)
                folded(eng.tensor_copy(w_inT[:, :, :].rearrange("p j n -> p (j n)"), bank_a[:, 0:DIN]))
                assert steps[0] == FOLD_TURNED

            def fold_mix():
                eng.wait_ge(s_fold_p, 3)
                folded(eng.tensor_copy(w_z[:, :], bank_d[:, 0:DIN]))
                eng.wait_ge(s_load_mix, 16 * MIX_LOADS)
                folded(eng.tensor_tensor(b_z[:, :], bank_c[:, 0:FB], b_g_c[:, :], ALU.add))
                eng.wait_ge(s_fold_v, steps[0])
                folded(eng.tensor_scalar(b_z_half[:, :], b_z[:, :], 0.5, None, ALU.mult))
                for j in range(FB):
                    folded(eng.tensor_scalar(w_outs[:, j, :], w_out[:, j, :], b_sp_c[:, j:j + 1], None, ALU.mult))
                assert steps[0] == FOLD_MIX
                eng.memset(k_stack[0][64:STACK_ROWS, :, :].bitcast(F32), TWO_ONES).then_inc(s_set, 1)

            def fold_gains():
                eng.wait_ge(s_load, 16 * LOADS)
                eng.wait_ge(s_const, 4)
                for w in range(3):
                    to = w_qkvs[:, w, :]
                    of = w_qkv[:, w, :]
                    if w < 2:
                        of = of.rearrange("p (h d) -> p d h", d=DK)
                        to = to.rearrange("p (d h) -> p d h", d=DK)
                    folded(eng.tensor_scalar(to, of, g1_c[:, 0:1], SCALE if w == 0 else 1.0, ALU.mult, ALU.mult))
                folded(eng.tensor_scalar(w_1s[:, :], w_1[:, :, :].rearrange("p e h -> p (e h)"), g2_c[:, 0:1], None,
                                         ALU.mult))
                folded(eng.memset(w_gates[:, E:GATE_COLS], 0.0))
                folded(eng.tensor_scalar(w_gates[:, 0:E], w_gate[:, :], g2_c[:, 0:1], None, ALU.mult))
                folded(eng.tensor_scalar(b2_wide[:, :], ones[:, :], b2_c[:, 0:1], None, ALU.mult))
                for w in range(2):
                    folded(eng.tensor_scalar(x2[:, 0, w, :].rearrange("p (d h) -> p d h", d=DK),
                                             w_qkv[:, w, :].rearrange("p (h d) -> p d h", d=DK), 1.0, None,
                                             ALU.mult))
                assert steps[0] == FOLD_READY

            def fold_columns():
                eng.wait_ge(s_fold_p, 4)
                folded(eng.tensor_copy(b_v[:, :], bank_d[:, 0:1]))
                eng.wait_ge(s_fold_v, steps[0])
                folded(eng.tensor_scalar(b_v_wide[:, :], ones[:, :], b_v[:, 0:1], None, ALU.mult))
                assert steps[0] == FOLD_V_WIDE
                folded(eng.tensor_scalar(b_qk[:, 0:1], bank_c[:, 0:1], SCALE, None, ALU.mult))
                folded(eng.tensor_copy(b_qk[:, 1:2], bank_c[:, 1:2]))
                folded(eng.tensor_copy(b_1[:, :], bank_c[:, 2:2 + HB]))

            def fold_rows():
                eng.wait_ge(s_fold_p, 5)
                folded(eng.tensor_copy(c_row[:, :], bank_s[0][:, 0:D]))
                folded(eng.tensor_copy(b_gate_r[:, :], bank_s[0][:, D:D + E]))
                assert steps[0] == FOLD_V
                eng.wait_ge(s_fold_v, FOLD_V)

            def stats(src, st, st_ok):
                for t in range(TT):
                    eng.bn_stats(st[:, t, :], src[:, t, :]).then_inc(st_ok.sem, 1)

            def moments(st, st_ok, mv, ok, b):
                for t in range(TT):
                    eng.wait_ge(st_ok.sem, st_ok.at(b, t + 1))
                    carry(eng, b)
                    eng.bn_aggr(mv[:, t, :], st[:, t, :]).then_inc(ok.sem, 1)

            def centred(to, src, mv, rs, ok, b):
                for t in range(TT):
                    eng.tensor_scalar(to[:, t, :], src[:, t, :], mv[:, t, 0:1], rs[:, t:t + 1],
                                      ALU.subtract, ALU.mult).then_inc(ok.sem, 1)

            def epsilon(ve, mv, ok, mv_ok, read, b):
                if b.past(1):
                    eng.wait_ge(read.sem, read.at(b.ago(1)))
                eng.wait_ge(mv_ok.sem, mv_ok.at(b))
                eng.tensor_scalar(ve[:, :], mv[:, :, 1], EPS, None, ALU.add).then_inc(ok.sem, 1)

            def slot(at):
                for h in range(HEADS):
                    b = at(0)
                    if b and h == 2:
                        max_low(b, 1)
                    b = at(1)
                    if b and h == 11:
                        max_low(b, 0)
                    b = at(-1)
                    if b:
                        if h == 4:
                            tok = bank_c[:, :].rearrange("p (t h c) -> p t h c", t=TT, c=SPAN)
                            eng.wait_ge(tok_up.sem, tok_up.at(b))
                            eng.reciprocal(r_sum[:, :, :], tok[:, :, :, DK]).then_inc(rs_ok.sem, 1)
                            eng.wait_ge(rs_ok.sem, rs_ok.at(b))
                            if b.past(1):
                                eng.wait_ge(onT_up.sem, onT_up.at(b.ago(1)))
                            eng.tensor_tensor(on[:, :, :, :].rearrange("p t h d -> p (t h) d"),
                                              tok[:, :, :, 0:DK].rearrange("p t h d -> p (t h) d"),
                                              r_sum[:, :, :].rearrange("p t (h o) -> p (t h) o", o=1)
                                              .broadcast_to([P, TT * HEADS, DK]), ALU.mult).then_inc(on_ok.sem, 1)
                        if h == 9:
                            eng.wait_ge(att_up.sem, att_up.at(b))
                            eng.wait_ge(L3c_ok.sem, L3c_ok.at(b))
                            if b.past(2):
                                eng.wait_ge(n4_ok.sem, n4_ok.at(b.ago(2)))
                                eng.wait_ge(x12_ok.sem, x12_ok.at(b.ago(2)))
                            eng.tensor_tensor(x2[:, b.turnof(2), :, :].rearrange("p t d -> p (t d)"),
                                              bank_c[:, 0:TT * D],
                                              L3c[:, b.turnof(4), :, :].rearrange("p t d -> p (t d)"), ALU.add)\
                               .then_inc(x2_ok.sem, 1)
                    b = at(4)
                    if b:
                        k = b.turnof(2)
                        if h == 8:
                            if b.past(1):
                                eng.wait_ge(o_up.sem, o_up.at(b.ago(1)))
                            eng.wait_ge(th_ok.sem, th_ok.at(b))
                            for f in range(FB):
                                eng.wait_ge(sg_ok.sem, sg_ok.at(b, f + 1))
                                eng.scalar_tensor_tensor(gT[:, f, :], bank_a[:, f * N:(f + 1) * N], b_z[:, f:f + 1],
                                                         sg[:, f, :], ALU.add, ALU.mult).then_inc(gT_ok.sem, 1)
                        if h == 10:
                            eng.wait_ge(o_up.sem, o_up.at(b))
                            eng.wait_ge(Lb_ok.sem, Lb_ok.at(b))
                            if b.past(2):
                                eng.wait_ge(a_ok.sem, a_ok.at(b.ago(2)))
                            eng.tensor_tensor(r[:, k, :, :].rearrange("p t d -> p (t d)"), bank_a[:, 0:TT * D],
                                              Lb[:, :, :].rearrange("p t d -> p (t d)"), ALU.add)\
                               .then_inc(r_ok.sem, 1)
                    b = at(-3)
                    if b and h == 15:
                        eng.wait_ge(y_up.sem, y_up.at(b))
                        eng.wait_ge(x12_ok.sem, x12_ok.at(b))
                        if b.past(1):
                            eng.wait_ge(o_out.sem, o_out.at(b.ago(1)))
                        eng.tensor_tensor(ob[:, :, :].rearrange("p t d -> p (t d)"), bank_d[:, 0:TT * D],
                                          x12[:, b.turnof(4), :, :].rearrange("p t d -> p (t d)"), ALU.add)\
                           .then_inc(ob_ok.sem, 1)
                    b = at(-2)
                    if b and h == 3:
                        eng.wait_ge(gate_up.sem, gate_up.at(b))
                        if b.past(1):
                            eng.wait_ge(at_ok.sem, at_ok.at(b.ago(1)))
                        for t in range(TT):
                            ins = eng.tensor_tensor(gate[:, t, :], bank_d[:, t * GATE_COLS:t * GATE_COLS + E],
                                                    b_gate_r[:, :], ALU.add)
                        ins.then_inc(gate_ok.sem, 1)
                    b = at(4)
                    if b and h == 0:
                        eng.wait_ge(x_in[b.turnof(2)].sem, x_in[b.turnof(2)].at(b))
                        stats(xin[:, b.turnof(2)], stats1, st1)
                    if b and h == 2:
                        eng.wait_ge(rstd1_ok.sem, rstd1_ok.at(b))
                        if b.past(2):
                            eng.wait_ge(Lb_ok.sem, Lb_ok.at(b.ago(2)))
                            eng.wait_ge(LT_up.sem, LT_up.at(b.ago(2)))
                        centred(L[:, b.turnof(2)], xin[:, b.turnof(2)], mv1, rstd1, L_ok, b)
                    b = at(1)
                    if b:
                        eng.wait_ge(m_up.sem, m_up.at(b, h + 1))
                        if h == 0:
                            if b.past(2):
                                eng.wait_ge(mT_up.sem, mT_up.at(b.ago(2)))
                        eng.tensor_reduce(neg_max[:, b.turnof(2), h, :],
                                          bank_m[h % 2][:, :].rearrange("p (t n) -> p t n", t=TT), AX_X, ALU.max,
                                          negate=True).then_inc(m_ok.sem, 1)
                    b = at(-2)
                    if b:
                        if h == 10:
                            eng.wait_ge(atf_ok.sem, atf_ok.at(b))
                            eng.wait_ge(p2_ok.sem, p2_ok.at(b))
                            if b.past(1):
                                eng.wait_ge(mw_ok.sem, mw_ok.at(b.ago(1)))
                            for t in range(TT):
                                for n in range(2):
                                    eng.tensor_scalar(pick[:, n, t, :], iota_e[:, :], top_atf[:, t, n:n + 1],
                                                      prob2[:, n, t:t + 1], ALU.is_equal, ALU.mult)\
                                       .then_inc(pick_ok.sem, 1)
                        if h == 11:
                            eng.wait_ge(pick_ok.sem, pick_ok.at(b))
                            if b.past(1):
                                eng.wait_ge(mwT_up.sem, mwT_up.at(b.ago(1)))
                            eng.tensor_tensor(mix_w[:, :, :].rearrange("p e t -> p t e"), pick[:, 0, :, :],
                                              pick[:, 1, :, :], ALU.add)\
                               .then_inc(mw_ok.sem, 1)
                    b = at(4)
                    if b and b.turn is None and b.offset == 0:
                        if h == 2:
                            fold_mix()
                    if b and b.turn is None and b.offset == 1:
                        if h == 3:
                            fold_columns()
                        if h == 6:
                            fold_rows()
                    if b:
                        k = b.turnof(2)
                        if h == 0:
                            if b.past(1):
                                eng.wait_ge(ve1_ok.sem, ve1_ok.at(b.ago(1)))
                                eng.wait_ge(L_ok.sem, L_ok.at(b.ago(1)))
                            moments(stats1, st1, mv1, mv1_ok, b)
                            epsilon(ve1, mv1, ve1_ok, mv1_ok, rstd1_ok, b)
                        if h == 13:
                            if b.past(1):
                                eng.wait_ge(ve2_ok.sem, ve2_ok.at(b.ago(1)))
                                eng.wait_ge(a_ok.sem, a_ok.at(b.ago(1)))
                            moments(stats2, st2, mv2, mv2_ok, b)
                        if h == 14:
                            epsilon(ve2, mv2, ve2_ok, mv2_ok, rstd2_ok, b)
                            if b.turn is None and b.offset == 0:
                                fold_gains()
                    b = at(3)
                    if b:
                        k = b.turnof(2)
                        if h == 5:
                            eng.wait_ge(x1_ok.sem, x1_ok.at(b))
                            stats(x1[:, k], stats3, st3)
                        if h == 6:
                            if b.past(2):
                                eng.wait_ge(n3_ok.sem, n3_ok.at(b.ago(2)))
                                eng.wait_ge(L3_ok.sem, L3_ok.at(b.ago(2)))
                            moments(stats3, st3, mv3[:, k], mv3_ok, b)
                        if h == 7:
                            if b.past(1):
                                eng.wait_ge(rstd3_ok.sem, rstd3_ok.at(b.ago(1)))
                            eng.wait_ge(mv3_ok.sem, mv3_ok.at(b))
                            eng.tensor_scalar(ve3[:, 0, :], mv3[:, k, :, 1], EPS, None, ALU.add)\
                               .then_inc(ve3_ok.sem, 1)
                            eng.tensor_scalar(ve3[:, 1, :], mv3[:, k, :, 1], 1.0 + EPS, EPS * EPS, ALU.mult, ALU.add)\
                               .then_inc(ve3_ok.sem, 1)
                        if h == 9:
                            eng.wait_ge(rstd3_ok.sem, rstd3_ok.at(b))
                            if b.past(1):
                                eng.wait_ge(nT_up.sem, nT_up.at(b.ago(1)))
                            centred(n3, x1[:, k], mv3[:, k], rstd3[:, k, 1], n3_ok, b)
                        if h == 13:
                            if b.past(2):
                                eng.wait_ge(L3_ok.sem, L3_ok.at(b.ago(2)))
                            eng.scalar_tensor_tensor(shift3[:, k, :], mv3[:, k, :, 0], -1.0, rstd3[:, k, 0, :],
                                                     ALU.mult, ALU.mult).then_inc(shift3_ok.sem, 1)
                    b = at(-1)
                    if b:
                        if h == 11:
                            eng.wait_ge(x2_ok.sem, x2_ok.at(b))
                            stats(x2[:, b.turnof(2)], stats4, st4)
                        if h == 12:
                            if b.past(1):
                                eng.wait_ge(ve4_ok.sem, ve4_ok.at(b.ago(1)))
                                eng.wait_ge(n4_ok.sem, n4_ok.at(b.ago(1)))
                            moments(stats4, st4, mv4, mv4_ok, b)
                    b = at(4)
                    if b and h == 12:
                        eng.wait_ge(r_ok.sem, r_ok.at(b))
                        stats(r[:, b.turnof(2)], stats2, st2)
                    b = at(-1)
                    if b:
                        if h == 12:
                            epsilon(ve4, mv4, ve4_ok, mv4_ok, rstd4_ok, b)
                        if h == 14:
                            eng.wait_ge(rstd4_ok.sem, rstd4_ok.at(b))
                            if b.past(1):
                                eng.wait_ge(n4T_up.sem, n4T_up.at(b.ago(1)))
                            centred(n4, x2[:, b.turnof(2)], mv4, rstd4, n4_ok, b)
                    b = at(-2)
                    if b:
                        if h == 3:
                            eng.wait_ge(gate_ok.sem, gate_ok.at(b))
                            carry(eng, b)
                            for t in range(TT):
                                eng.max(top[:, t, :], gate[:, t, :]).then_inc(top_ok.sem, 1)
                        if h == 4:
                            for t in range(TT):
                                eng.wait_ge(top_ok.sem, top_ok.at(b, t + 1))
                                carry(eng, b)
                                eng.max_index(top_at[:, t, :], top[:, t, :], gate[:, t, :]).then_inc(at_ok.sem, 1)
                            if b.past(1):
                                eng.wait_ge(eg_ok.sem, eg_ok.at(b.ago(1)))
                            eng.tensor_tensor(gap[:, :], top[:, :, 1], top[:, :, 0], ALU.subtract)\
                               .then_inc(gap_ok.sem, 1)
                        if h == 6:
                            eng.wait_ge(at_ok.sem, at_ok.at(b))
                            if b.past(1):
                                eng.wait_ge(pick_ok.sem, pick_ok.at(b.ago(1)))
                            eng.tensor_copy(top_atf[:, :, :], top_at[:, :, :]).then_inc(atf_ok.sem, 1)
                        if h == 6:
                            eng.wait_ge(eg_ok.sem, eg_ok.at(b))
                            eng.tensor_scalar(denom[:, :], e_gap[:, :], 1.0, None, ALU.add).then_inc(den_ok.sem, 1)
                            eng.wait_ge(den_ok.sem, den_ok.at(b))
                            eng.reciprocal(prob2[:, 0, :], denom[:, :]).then_inc(p1_ok.sem, 1)
                        if h == 7:
                            eng.wait_ge(p1_ok.sem, p1_ok.at(b))
                            eng.tensor_tensor(prob2[:, 1, :], prob2[:, 0, :], e_gap[:, :], ALU.mult)\
                               .then_inc(p2_ok.sem, 1)

            def max_low(b, half):
                eng.wait_ge(mhi_ok.sem, mhi_ok.at(b, half + 1))
                if b.past(1):
                    eng.wait_ge(shift_in[half][b.turnof(2) ^ 1].sem, shift_in[half][b.turnof(2) ^ 1].at(b.ago(1)))
                eng.tensor_tensor(max_lo[:, half, :], bank_c[0:HEADS // 2 * TT, 0:P], max_hi[:, half, :],
                                  ALU.subtract).then_inc(mlo_ok.sem, 1)

            fold_turned()
            slots(eng, slot)

        @block.tensor
        def _(eng):
            eng.wait_ge(s_load_z, 16 * Z_LOADS)
            eng.wait_ge(s_const, 4)
            for j in range(FB):
                ins = eng.transpose(bank_a[:, j * P:(j + 1) * P], w_in[:, j * P:(j + 1) * P], ident[:, :])
            ins.then_inc(s_fold_p, 1)
            for f in range(FB):
                for j in range(FB):
                    ins = eng.matmul(bank_c[:, f:f + 1], w_g[:, j, f * P:(f + 1) * P], b_in_c[:, j:j + 1],
                                     start=(j == 0), stop=(j == FB - 1))
            ins.then_inc(s_fold_p, 1)
            eng.wait_ge(s_fold_v, FOLD_TURNED)
            for j in range(FB):
                ins = eng.matmul(bank_d[:, 0:DIN], w_inT[:, j, :], w_g[:, j, :], start=(j == 0), stop=(j == FB - 1))
            ins.then_inc(s_fold_p, 1)

            def fold_columns():
                eng.wait_ge(s_fold_v, FOLD_READY)
                ins = eng.matmul(bank_d[:, 0:1], w_qkv[:, 2, :], b1_c[:, 0:1], start=True, stop=True)
                for w in range(2):
                    ins = eng.matmul(bank_c[:, w:w + 1], x2[:, 0, w, :], b1_c[:, 0:1], start=True, stop=True)
                for j in range(HB):
                    ins = eng.matmul(bank_c[:, 2 + j:3 + j],
                                     w_1[:, :, :].rearrange("p e h -> p (e h)")[:, j * P:(j + 1) * P],
                                     b2_c[:, 0:1], start=True, stop=True)
                ins.then_inc(s_fold_p, 1)

            def fold_rows():
                eng.wait_ge(s_fold_v, FOLD_V_WIDE)
                ins = eng.matmul(bank_s[0][:, 0:D], b_v_wide[:, :], w_o[:, :], start=True, stop=True)
                ins = eng.matmul(bank_s[0][:, D:D + E], b2_wide[:, :], w_gate[:, :], start=True, stop=True)
                ins.then_inc(s_fold_p, 1)

            def slot(at):
                for h in range(HEADS):
                    b = at(0)
                    if b:
                        k = b.turnof(4)
                        if h % (HEADS // 2) == 0:
                            half = h // (HEADS // 2)
                            eng.wait_ge(shift_in[half][b.turnof(2)].sem, shift_in[half][b.turnof(2)].at(b))
                        if b.past(1) or h - 1 > 0:
                            eng.wait_ge(p_ok.sem, p_ok.at(b, h - 1))
                        for t in range(TT):
                            ins = eng.matmul(bank_s[h % 2][:, t * N:(t + 1) * N],
                                             k_stack[k][:, ORDER[h], t * P:(t + 1) * P], q_stack[k][:, ORDER[h], :],
                                             start=True, stop=True)
                        ins.then_inc(s_up.sem, 1)
                    b = at(1)
                    if b:
                        k = b.turnof(4)
                        if h == 0:
                            eng.wait_ge(stacked[b.turnof(2)].sem, stacked[b.turnof(2)].at(b))
                            if b.turn is None and b.offset == 0:
                                eng.wait_ge(s_zero, SET_POOL)
                        if b.past(1) or h - 1 > 0:
                            eng.wait_ge(m_ok.sem, m_ok.at(b, h - 1))
                        for t in range(TT):
                            ins = eng.matmul(bank_m[h % 2][:, t * N:(t + 1) * N],
                                             q_stack[k][0:SHIFT_ROW, h, t * P:(t + 1) * P],
                                             k_stack[k][0:SHIFT_ROW, h, :], start=True, stop=True)
                        ins.then_inc(m_up.sem, 1)
                    b = at(0)
                    if b:
                        if h == 1:
                            turn_max(b, 1, at)
                        if h in WEIGH_AT:
                            weigh(b, WEIGH_AT.index(h))
                    b = at(-1)
                    if b:
                        if h == 1:
                            weigh(b, GROUPS - 1)
                        if h == 3:
                            eng.wait_ge(oT_ok.sem, oT_ok.at(b))
                            if at(0):
                                eng.wait_ge(mlo_ok.sem, mlo_ok.at(b.ago(-1)))
                            else:
                                eng.wait_ge(x2_ok.sem, x2_ok.at(b.ago(1)))
                            for t in range(TT):
                                for u in range(2):
                                    ins = eng.transpose(bank_c[:, (2 * t + u) * P:(2 * t + u + 1) * P],
                                                        oT[:, u, t * P:(t + 1) * P], ident[:, :])
                            ins.then_inc(tok_up.sem, 1)
                        if h == 5:
                            eng.wait_ge(on_ok.sem, on_ok.at(b))
                            for t in range(TT):
                                ins = eng.transpose(bank_c[:, t * P:(t + 1) * P],
                                                    on[:, t, :, :].rearrange("p h d -> p (h d)"), ident[:, :])
                            ins.then_inc(onT_up.sem, 1)
                    b = at(1)
                    if b and h == 10:
                        turn_max(b, 0, at)
                    b = at(-1)
                    if b and h == 8:
                        eng.wait_ge(onT_ok.sem, onT_ok.at(b))
                        for t in range(TT):
                            ins = eng.matmul(bank_c[:, t * D:(t + 1) * D], onT[:, t * P:(t + 1) * P], w_o[:, :],
                                             start=True, stop=True)
                        ins.then_inc(att_up.sem, 1)
                    b = at(4)
                    if b and b.turn is None and b.offset == 1:
                        if h == 0:
                            fold_columns()
                        if h == 4:
                            fold_rows()
                    if b:
                        k = b.turnof(2)
                        if h == 3:
                            eng.wait_ge(L_ok.sem, L_ok.at(b))
                            LT_free(b, at)
                            for t in range(TT):
                                ins = eng.transpose(bank_a[:, t * P:(t + 1) * P], L[:, k, t, :], ident[:, :])
                            ins.then_inc(LT_up.sem, 1)
                        if h == 5:
                            eng.wait_ge(LT_ok.sem, LT_ok.at(b))
                            if b.turn is None and b.offset == 0:
                                eng.wait_ge(s_fold_v, FOLD_TURNED + 1)
                            for f in range(FB):
                                ins = eng.matmul(bank_a[:, f * N:(f + 1) * N], w_z[:, f * P:(f + 1) * P], LT[:, :],
                                                 start=True, stop=True)
                            ins.then_inc(z_up.sem, 1)
                        if h == 9:
                            eng.wait_ge(gT_ok.sem, gT_ok.at(b))
                            for t in range(TT):
                                for f in range(FB):
                                    ins = eng.matmul(bank_a[:, t * D:(t + 1) * D], gT[:, f, t * P:(t + 1) * P],
                                                     w_outs[:, f, :], start=(f == 0), stop=(f == FB - 1))
                            ins.then_inc(o_up.sem, 1)
                    b = at(3)
                    if b:
                        if h == 11:
                            eng.wait_ge(n3_ok.sem, n3_ok.at(b))
                            if at(4):
                                eng.wait_ge(r_ok.sem, r_ok.at(b.ago(-1)))
                            else:
                                if b.past(1):
                                    eng.wait_ge(qk_ok.sem, qk_ok.at(b.ago(1)))
                            for t in range(TT):
                                ins = eng.transpose(bank_a[:, t * P:(t + 1) * P], n3[:, t, :], ident[:, :])
                            ins.then_inc(nT_up.sem, 1)
                        if h == 13:
                            eng.wait_ge(nT_ok.sem, nT_ok.at(b))
                            for w in range(2):
                                ins = eng.matmul(bank_a[:, w * N:(w + 1) * N], w_qkvs[:, w, :], nT[:, :],
                                                 start=True, stop=True)
                            ins.then_inc(qk_up.sem, 1)
                        if h == 15:
                            if b.past(1):
                                eng.wait_ge(v_ok.sem, v_ok.at(b.ago(1)))
                            else:
                                eng.wait_ge(s_fold_v, FOLD_V)
                            if b.past(2):
                                eng.wait_ge(mlo_ok.sem, mlo_ok.at(b.ago(2), 1))
                            for t in range(TT):
                                ins = eng.matmul(bank_c[:, t * D:(t + 1) * D], nT[:, t * P:(t + 1) * P],
                                                 w_qkvs[:, 2, :], start=True, stop=True)
                            ins.then_inc(v_up.sem, 1)
                    b = at(-2)
                    if b:
                        k = b.turnof(2)
                        if h == 0:
                            eng.wait_ge(n4_ok.sem, n4_ok.at(b))
                            if b.past(2):
                                eng.wait_ge(ob_ok.sem, ob_ok.at(b.ago(2)))
                            elif b.past(1):
                                eng.wait_ge(mwT_ok.sem, mwT_ok.at(b.ago(1)))
                            for t in range(TT):
                                ins = eng.transpose(bank_d[:, t * P:(t + 1) * P], n4[:, t, :], ident[:, :])
                            ins.then_inc(n4T_up.sem, 1)
                        if h == 2:
                            eng.wait_ge(n4T_ok.sem, n4T_ok.at(b))
                            for t in range(TT):
                                ins = eng.matmul(bank_d[:, t * GATE_COLS:(t + 1) * GATE_COLS],
                                                 n4T[:, k, t * P:(t + 1) * P], w_gates[:, :], start=True, stop=True)
                            ins.then_inc(gate_up.sem, 1)
                    b = at(-2)
                    if b:
                        if h in (4, 6):
                            j0 = h - 4
                            if j0:
                                eng.wait_ge(h_ok.sem, h_ok.at(b, 2))
                            else:
                                eng.wait_ge(gate_ok.sem, gate_ok.at(b))
                            for j in (j0, j0 + 1):
                                ins = eng.matmul(bank_d[:, (j - j0) * N:(j - j0 + 1) * N],
                                                 w_1s[:, j * P:(j + 1) * P], n4T[:, b.turnof(2), :],
                                                 start=True, stop=True)
                            ins.then_inc(h_up.sem, 1)
                    b = at(-2)
                    if b:
                        if h == 12:
                            eng.wait_ge(mw_ok.sem, mw_ok.at(b))
                            eng.wait_ge(h_ok.sem, h_ok.at(b))
                            ins = eng.transpose(bank_d[0:E * TT, 0:P], mix_w[:, :, :].rearrange("p e t -> p (e t)"),
                                                ident[:, :])
                            ins.then_inc(mwT_up.sem, 1)
                    b = at(-3)
                    if b and h in (13, 14):
                        t = h - 13
                        eng.wait_ge(hw_ok.sem, hw_ok.at(b, t + 1))
                        if t == 0:
                            if at(-2):
                                eng.wait_ge(mwT_ok.sem, mwT_ok.at(b.ago(-1)))
                            else:
                                eng.wait_ge(ob_ok.sem, ob_ok.at(b.ago(1)))
                        for j in range(HB):
                            ins = eng.matmul(bank_d[:, t * D:(t + 1) * D], hidw[:, j, t * P:(t + 1) * P],
                                             w_2[:, j, :], start=(j == 0), stop=(j == HB - 1))
                        ins.then_inc(y_up.sem, 1)

            def LT_free(b, at):
                if b.past(2):
                    eng.wait_ge(qk_ok.sem, qk_ok.at(b.ago(2)))
                elif b.past(1):
                    eng.wait_ge(r_ok.sem, r_ok.at(b.ago(1)))

            def turn_max(b, half, at):
                eng.wait_ge(m_ok.sem, m_ok.at(b, (half + 1) * (HEADS // 2)))
                if half == 0:
                    if b.past(2):
                        eng.wait_ge(x2_ok.sem, x2_ok.at(b.ago(2)))
                    elif b.past(1):
                        eng.wait_ge(mlo_ok.sem, mlo_ok.at(b.ago(1)))
                    else:
                        eng.wait_ge(v_ok.sem, v_ok.at(b.ago(-1)))
                else:
                    eng.wait_ge(mlo_ok.sem, mlo_ok.at(b, 1))
                    if at(2):
                        eng.wait_ge(v_ok.sem, v_ok.at(b.ago(-2)))
                k = b.turnof(2)
                hs = slice(half * (HEADS // 2), (half + 1) * (HEADS // 2))
                ins = eng.transpose(bank_c[0:HEADS // 2 * TT, 0:P],
                                    neg_max[:, k, hs, :].rearrange("p h t -> p (h t)"), ident[:, :])
                ins.then_inc(mT_up.sem, 1)

            def weigh(b, g):
                k = b.turnof(4)
                eng.wait_ge(p_ok.sem, p_ok.at(b, GROUP * (g + 1)))
                eng.wait_ge(v_ok.sem, v_ok.at(b))
                u, odd = g // 2, g % 2 == 1
                if not odd:
                    if b.past(1) or g // 2 > 0:
                        eng.wait_ge(oT_ok.sem, oT_ok.at(b, g // 2))
                for t in range(TT):
                    for j in range(GROUP):
                        h = GROUP * g + j
                        ins = eng.matmul(bank_o[32 * j:32 * (j + 1), u * N:(u + 1) * N],
                                         v_one[:, k, t, ORDER[h], :], probs[:, h % P_RING, t, :],
                                         start=(not odd and t == 0), stop=(odd and t == TT - 1))
                ins.then_inc(pv_up.sem, 1)

            slots(eng, slot)


TWO_ONES = 1.0 + 0x3F80 / 2 ** 23
Z_LOADS = 3
MIX_LOADS = 6
LOADS = 11
FOLD_TURNED = 1
FOLD_MIX = 6
FOLD_READY = 15
FOLD_V_WIDE = 17
FOLD_V = 22
SET_POOL = 6


_INS = ["L0_attn_x", "L0_attn_W_in", "L0_attn_b_in", "L0_attn_b_sp", "L0_attn_W_g", "L0_attn_b_g", "L0_attn_W_out",
        "L0_attn_b_out", "L0_attn_norm_w", "L0_attn_norm_b", "L0_ffn_Wq", "L0_ffn_Wk", "L0_ffn_Wv", "L0_ffn_Wo",
        "L0_ffn_g1", "L0_ffn_b1", "L0_ffn_g2", "L0_ffn_b2", "L0_ffn_Wg", "L0_ffn_W1", "L0_ffn_W2"]


def kernel(**inputs):
    import numpy as _np
    import concourse.bacc as _bacc
    from concourse import mybir as _mybir
    from concourse.bass_utils import run_bass_kernel_spmd as _run

    nc = _bacc.Bacc("TRN2", target_bir_lowering=False, num_devices=1)
    arrays, args = {}, []
    for name in _INS:
        v = _np.ascontiguousarray(inputs[name])
        arrays[f"in_{name}_dram"] = v
        args.append(nc.dram_tensor(f"in_{name}_dram", v.shape, _mybir.dt.from_np(v.dtype), kind="ExternalInput").ap())
    shape = inputs["L0_attn_x"].shape
    args.append(nc.dram_tensor("out_0_dram", shape, _mybir.dt.float32, kind="ExternalOutput").ap())
    build(nc, *args)
    got = _run(nc, [arrays], core_ids=[0])
    return got.results[0]["out_0_dram"]
```
